# Optimizing a Trainium2 kernel written in Bass

```python
import numpy as np
import jax
import jax.numpy as jnp

def _softmax(x, axis=-1):
    return jax.nn.softmax(x, axis=axis)

def _gelu(x):
    return jax.nn.gelu(x, approximate=True)

def _silu(x):
    return jax.nn.silu(x)

def _sigmoid(x):
    return jax.nn.sigmoid(x)

def _layernorm(x, axis=-1, eps=1e-05):
    m = jnp.mean(x, axis=axis, keepdims=True)
    v = jnp.var(x, axis=axis, keepdims=True)
    return (x - m) / jnp.sqrt(v + eps)

def _scatter_add(tgt, idx, src, axis=0):
    return tgt.at[idx].add(src)

def _segment_sum(src, seg, n):
    return jax.ops.segment_sum(src, seg, n)
kernel_name = 'mk_flamingo_gated_d2_seqx_r4_bf2016'

def setup_inputs(seed: int=0):
    np.random.seed(seed)
    _w = jnp.asarray

    def _rec_inputs():
        import jax
        import jax.numpy as jnp
        _rk = jax.random.key(seed)
        x = -0.0002928 + 1 * jax.random.normal(jax.random.fold_in(_rk, 1), (16, 256, 256), jnp.float32)
        _lenS = 256 - jax.random.randint(jax.random.fold_in(_rk, 7), (16,), 0, max(1, 256 // 4) + 1, jnp.int32)
        _lenS2 = 77 - jax.random.randint(jax.random.fold_in(_rk, 8), (16,), 0, max(1, 77 // 4) + 1, jnp.int32)
        _ctx_1024P = jax.random.normal(jax.random.fold_in(_rk, 11), (16, 16, 256), jnp.float32)
        _ctx_1024c = jax.random.dirichlet(jax.random.fold_in(_rk, 511), 0.3 * jnp.ones((16,), jnp.float32), (16, 77))
        _ctx_1024t = jnp.einsum('bsk,bkd->bsd', _ctx_1024c, _ctx_1024P)
        _ctx_1024t = _ctx_1024t * jax.lax.rsqrt(jnp.mean(jnp.square(_ctx_1024t)) + 1e-12) * 0.953939
        ctx_1024 = -1.39393e-06 + 0.999914 * (_ctx_1024t + 0.3 * jax.random.normal(jax.random.fold_in(_rk, 611), (16, 77, 256), jnp.float32))
        _validS = jnp.arange(256)[None, :] < _lenS[:, None]
        _validS2 = jnp.arange(77)[None, :] < _lenS2[:, None]
        _causal = jnp.tril(jnp.ones((256, 256), dtype=bool))
        mask_BxSxS2_ff0 = jnp.where(jnp.ones((16, 256, 77), dtype=bool), 0.0, -1000000000.0).astype(jnp.float32)
        _g = jax.random.normal(jax.random.fold_in(_rk, 9001), (2, 2), jnp.float32)
        _g = jnp.sign(_g) * jnp.maximum(jnp.abs(_g), 1.0) + (_g == 0) * 1.0
        g_xattn = _g[0]
        g_ffn = _g[1]
        return (x, ctx_1024, mask_BxSxS2_ff0, g_xattn, g_ffn)
    x, ctx_1024, mask_BxSxS2_ff0, g_xattn, g_ffn = _rec_inputs()

    def _L0_xattn_setup():
        import jax, jax.numpy as jnp
        import numpy as np
        HEADS = 16
        MASK_VAL = 1000000000000.0
        key = jax.random.key(seed)
        ks = jax.random.split(key, 6)
        B, S, F = (2, 512, 256)
        scale = 1.0 / np.sqrt(F)
        return {'attend_from': jax.random.normal(ks[0], (B, S, F), jnp.float32), 'attend_to': jax.random.normal(ks[1], (B, S, F), jnp.float32), 'w_q': jax.random.normal(ks[2], (F, F), jnp.float32) * scale, 'b_q': jnp.zeros((F,), jnp.float32), 'w_kv': jax.random.normal(ks[3], (F, 2 * F), jnp.float32) * scale, 'b_kv': jnp.zeros((2 * F,), jnp.float32), 'w_out': jax.random.normal(ks[4], (F, F), jnp.float32) * scale, 'b_out': jnp.zeros((F,), jnp.float32)}
    _L0_xattn_all = _L0_xattn_setup()
    _L0_xattn_in = {k: v for k, v in _L0_xattn_all.items() if k in ('w_q', 'b_q', 'w_kv', 'b_kv', 'w_out', 'b_out')}
    del _L0_xattn_all

    def _L0_ffn_setup():
        import jax, jax.numpy as jnp
        import numpy as np
        E, H, I = (8, 256, 1024)
        B, S = (4, 512)
        key = jax.random.key(seed)
        k0, k1, k2, k3 = jax.random.split(key, 4)
        s = 0.02
        return {'hidden_states': jax.random.normal(k0, (B, S, H), dtype=jnp.float32), 'w1': jax.random.normal(k1, (E, H, I), dtype=jnp.float32) * s, 'b1': jnp.zeros((E, I), dtype=jnp.float32), 'w2': jax.random.normal(k2, (E, I, H), dtype=jnp.float32) * s, 'b2': jnp.zeros((E, H), dtype=jnp.float32), 'wr': jax.random.normal(k3, (H, E), dtype=jnp.float32) * s, 'br': jnp.zeros((E,), dtype=jnp.float32)}
    _L0_ffn_all = _L0_ffn_setup()
    _L0_ffn_in = {k: v for k, v in _L0_ffn_all.items() if k in ('w1', 'b1', 'w2', 'b2', 'wr', 'br')}
    del _L0_ffn_all

    def _L1_xattn_setup():
        import jax, jax.numpy as jnp
        import numpy as np
        B, S, D, H = (4, 512, 256, 8)
        DEPTH = D // H

        def _split_heads(x):
            b, s, _ = x.shape
            return x.reshape(b, s, H, DEPTH).transpose(0, 2, 1, 3)
        key = jax.random.key(seed)
        ks = jax.random.split(key, 8)
        sc = 1.0 / np.sqrt(D)
        return {'q': jax.random.normal(ks[0], (B, S, D), jnp.float32), 'k': jax.random.normal(ks[1], (B, S, D), jnp.float32), 'v': jax.random.normal(ks[2], (B, S, D), jnp.float32), 'mask': jnp.zeros((B, S, S), jnp.float32), 'wq_kernel': jax.random.normal(ks[3], (D, D), jnp.float32) * sc, 'wq_bias': jnp.zeros((D,), jnp.float32), 'wk_kernel': jax.random.normal(ks[4], (D, D), jnp.float32) * sc, 'wk_bias': jnp.zeros((D,), jnp.float32), 'wv_kernel': jax.random.normal(ks[5], (D, D), jnp.float32) * sc, 'wv_bias': jnp.zeros((D,), jnp.float32)}
    _L1_xattn_all = _L1_xattn_setup()
    _L1_xattn_in = {k: v for k, v in _L1_xattn_all.items() if k in ('wq_kernel', 'wq_bias', 'wk_kernel', 'wk_bias', 'wv_kernel', 'wv_bias')}
    del _L1_xattn_all

    def _L1_ffn_setup():
        import jax, jax.numpy as jnp
        import numpy as np
        H = 256
        I = 256
        E = 8
        key = jax.random.key(seed)
        ks = jax.random.split(key, 8)
        s = 0.02
        x = jax.random.normal(ks[0], (4, 512, H), dtype=jnp.float32)
        Wg = jax.random.normal(ks[1], (H, E), dtype=jnp.float32) * s
        bg = jnp.zeros((E,), dtype=jnp.float32)
        W1 = jax.random.normal(ks[2], (E, H, I), dtype=jnp.float32) * s
        b1 = jnp.zeros((E, I), dtype=jnp.float32)
        W2 = jax.random.normal(ks[3], (E, I, H), dtype=jnp.float32) * s
        b2 = jnp.zeros((E, H), dtype=jnp.float32)
        return {'x': x, 'Wg': Wg, 'bg': bg, 'W1': W1, 'b1': b1, 'W2': W2, 'b2': b2}
    _L1_ffn_all = _L1_ffn_setup()
    _L1_ffn_in = {k: v for k, v in _L1_ffn_all.items() if k in ('Wg', 'bg', 'W1', 'b1', 'W2', 'b2')}
    del _L1_ffn_all
    return {'x': x, 'ctx_1024': ctx_1024, 'mask_BxSxS2_ff0': mask_BxSxS2_ff0, 'g_xattn': g_xattn, 'g_ffn': g_ffn, 'L0_xattn_w_q': _L0_xattn_in['w_q'], 'L0_xattn_b_q': _L0_xattn_in['b_q'], 'L0_xattn_w_kv': _L0_xattn_in['w_kv'], 'L0_xattn_b_kv': _L0_xattn_in['b_kv'], 'L0_xattn_w_out': _L0_xattn_in['w_out'], 'L0_xattn_b_out': _L0_xattn_in['b_out'], 'L0_ffn_w1': _L0_ffn_in['w1'], 'L0_ffn_b1': _L0_ffn_in['b1'], 'L0_ffn_w2': _L0_ffn_in['w2'], 'L0_ffn_b2': _L0_ffn_in['b2'], 'L0_ffn_wr': _L0_ffn_in['wr'], 'L0_ffn_br': _L0_ffn_in['br'], 'L1_xattn_wq_kernel': _L1_xattn_in['wq_kernel'], 'L1_xattn_wq_bias': _L1_xattn_in['wq_bias'], 'L1_xattn_wk_kernel': _L1_xattn_in['wk_kernel'], 'L1_xattn_wk_bias': _L1_xattn_in['wk_bias'], 'L1_xattn_wv_kernel': _L1_xattn_in['wv_kernel'], 'L1_xattn_wv_bias': _L1_xattn_in['wv_bias'], 'L1_ffn_Wg': _L1_ffn_in['Wg'], 'L1_ffn_bg': _L1_ffn_in['bg'], 'L1_ffn_W1': _L1_ffn_in['W1'], 'L1_ffn_b1': _L1_ffn_in['b1'], 'L1_ffn_W2': _L1_ffn_in['W2'], 'L1_ffn_b2': _L1_ffn_in['b2']}

def reference(x, ctx_1024, mask_BxSxS2_ff0, g_xattn, g_ffn, L0_xattn_w_q, L0_xattn_b_q, L0_xattn_w_kv, L0_xattn_b_kv, L0_xattn_w_out, L0_xattn_b_out, L0_ffn_w1, L0_ffn_b1, L0_ffn_w2, L0_ffn_b2, L0_ffn_wr, L0_ffn_br, L1_xattn_wq_kernel, L1_xattn_wq_bias, L1_xattn_wk_kernel, L1_xattn_wk_bias, L1_xattn_wv_kernel, L1_xattn_wv_bias, L1_ffn_Wg, L1_ffn_bg, L1_ffn_W1, L1_ffn_b1, L1_ffn_W2, L1_ffn_b2):
    import jax
    import jax.numpy as jnp

    def _L0_xattn_ref(attend_from, attend_to, w_q, b_q, w_kv, b_kv, w_out, b_out):
        import jax, jax.numpy as jnp
        import numpy as np
        HEADS = 16
        MASK_VAL = 1000000000000.0
        B, S, F = attend_from.shape
        H = HEADS
        d = F // H
        Z = attend_to.shape[1]
        qry = (attend_from @ w_q + b_q).reshape(B, S, H, d)
        kv = attend_to @ w_kv + b_kv
        key, val = jnp.split(kv, 2, axis=-1)
        key = key.reshape(B, Z, H, d)
        val = val.reshape(B, Z, H, d)
        logits = jnp.einsum('bshd,bzhd->bhsz', qry, key)
        mask = jnp.triu(jnp.ones((S, Z), dtype=logits.dtype)) * MASK_VAL
        logits = logits - mask
        attn = jax.nn.softmax(logits, axis=-1)
        out = jnp.einsum('bhsz,bzhd->bshd', attn, val).reshape(B, S, F)
        return out @ w_out + b_out

    def _L0_ffn_ref(hidden_states, w1, b1, w2, b2, wr, br):
        import jax, jax.numpy as jnp
        import numpy as np
        E, H, I = (8, 256, 1024)
        B, S = (4, 512)
        b, s, h = hidden_states.shape
        x = hidden_states.reshape(-1, h)
        logits = x @ wr + br
        probs = jax.nn.softmax(logits, axis=-1)
        top_p, top_i = jax.lax.top_k(probs, 2)
        gate = top_p[:, 0] / (top_p[:, 0] + top_p[:, 1])
        top1 = top_i[:, 0]
        out = jnp.zeros_like(x)
        n_experts = w1.shape[0]
        for e in range(n_experts):
            hmid = jax.nn.gelu(x @ w1[e] + b1[e], approximate=False)
            hout = hmid @ w2[e] + b2[e]
            mask = top1 == e
            out = out + jnp.where(mask[:, None], hout * gate[:, None], 0.0)
        return out.reshape(b, s, h)

    def _L1_xattn_ref(q, k, v, mask, wq_kernel, wq_bias, wk_kernel, wk_bias, wv_kernel, wv_bias):
        import jax, jax.numpy as jnp
        import numpy as np
        B, S, D, H = (4, 512, 256, 8)
        DEPTH = D // H

        def _split_heads(x):
            b, s, _ = x.shape
            return x.reshape(b, s, H, DEPTH).transpose(0, 2, 1, 3)
        qp = q @ wq_kernel + wq_bias
        kp = k @ wk_kernel + wk_bias
        vp = v @ wv_kernel + wv_bias
        qh, kh, vh = (_split_heads(qp), _split_heads(kp), _split_heads(vp))
        scale = 1.0 / jnp.sqrt(jnp.asarray(DEPTH, qh.dtype))
        scores = jnp.einsum('bhsd,bhtd->bhst', qh, kh) * scale
        scores = scores + mask[:, None, :, :] * jnp.asarray(-1000000000.0, scores.dtype)
        attn = jax.nn.softmax(scores, axis=-1)
        out = jnp.einsum('bhst,bhtd->bhsd', attn, vh)
        return out.transpose(0, 2, 1, 3).reshape(q.shape[0], q.shape[1], D)

    def _L1_ffn_ref(x, Wg, bg, W1, b1, W2, b2):
        import jax, jax.numpy as jnp
        import numpy as np
        H = 256
        I = 256
        E = 8
        B, S, Hd = x.shape
        xf = x.reshape(-1, Hd)
        logits = xf @ Wg + bg
        gates = jax.nn.softmax(logits, axis=-1)
        idx = jnp.argmax(gates, axis=-1)
        h = jax.nn.gelu(jnp.einsum('th,ehi->tei', xf, W1) + b1, approximate=False)
        y = jnp.einsum('tei,eih->teh', h, W2) + b2
        out = jnp.take_along_axis(y, idx[:, None, None], axis=1)[:, 0, :]
        return out.reshape(B, S, Hd)
    x = x + jnp.tanh(g_xattn[0]) * _L0_xattn_ref(_layernorm(x, axis=-1), ctx_1024, L0_xattn_w_q, L0_xattn_b_q, L0_xattn_w_kv, L0_xattn_b_kv, L0_xattn_w_out, L0_xattn_b_out)
    x = x + jnp.tanh(g_ffn[0]) * _L0_ffn_ref(_layernorm(x, axis=-1), L0_ffn_w1, L0_ffn_b1, L0_ffn_w2, L0_ffn_b2, L0_ffn_wr, L0_ffn_br)
    x = x + jnp.tanh(g_xattn[1]) * _L1_xattn_ref(_layernorm(x, axis=-1), ctx_1024, ctx_1024, mask_BxSxS2_ff0, L1_xattn_wq_kernel, L1_xattn_wq_bias, L1_xattn_wk_kernel, L1_xattn_wk_bias, L1_xattn_wv_kernel, L1_xattn_wv_bias)
    x = x + jnp.tanh(g_ffn[1]) * _L1_ffn_ref(_layernorm(x, axis=-1), L1_ffn_Wg, L1_ffn_bg, L1_ffn_W1, L1_ffn_b1, L1_ffn_W2, L1_ffn_b2)
    return x

_drawn_inputs = setup_inputs


def setup_inputs(seed=0):
    import zlib

    import numpy as np

    out = dict(_drawn_inputs(seed))
    spreads = {'g_ffn': (-1.0, 0.6),
     'L0_xattn_b_q': (0.0, 0.1),
     'L0_xattn_b_kv': (0.0, 0.1),
     'L0_xattn_b_out': (0.0, 0.1),
     'L0_ffn_b1': (0.0, 0.516),
     'L0_ffn_b2': (0.0, 0.1),
     'L0_ffn_br': (0.0, 0.1),
     'L1_xattn_wq_bias': (0.0, 0.398),
     'L1_xattn_wk_bias': (0.0, 0.8),
     'L1_xattn_wv_bias': (0.0, 0.1),
     'L1_ffn_bg': (0.0, 0.1),
     'L1_ffn_b1': (0.0, 0.691),
     'L1_ffn_b2': (0.0, 0.1)}
    factors = {}
    for name, (base, spread) in spreads.items():
        noise = np.random.default_rng([zlib.crc32(name.encode()), seed]).standard_normal(out[name].shape)
        drawn = base * np.exp(spread * noise) if base else spread * noise
        out[name] = jnp.asarray(drawn.astype(out[name].dtype))
    for name, factor in factors.items():
        out[name] = (out[name] * factor).astype(out[name].dtype)
    return out
```

```python
from contextlib import ExitStack

import concourse.bass as bass
from concourse import mybir

ALU = mybir.AluOpType
ACT = mybir.ActivationFunctionType
F32 = mybir.dt.float32
BF16 = mybir.dt.bfloat16
I32 = mybir.dt.int32
AX = mybir.AxisListType.X

P = 128
NB, S, D, Z = 16, 256, 256, 77
NC = D // P
TPB = S // P
NT = NB * TPB
E = 8
SLOT_TILES = (NB * S + E * (P - 1)) // P
NSLOT = SLOT_TILES * P
EPS = 1e-5
RING = 3
HG = 4
GZ = HG * Z
RG = 4

ATT = {
    0: dict(H=16, hpc=8, units=4, mask_val=1e12),
    1: dict(H=8, hpc=4, units=2, mask_val=1e9),
}
FFN = {0: dict(I=1024, CW=512), 1: dict(I=256, CW=256)}


def wait(eng, sem, value):
    if isinstance(value, int) and value <= 0:
        return
    eng.wait_ge(sem, value)


class Chain:

    def __init__(self, eng, sem, per, apart=None):
        self.eng, self.sem, self.per, self.apart = eng, sem, per, apart

    def begin(self, step):
        self.base, self.k = step * self.per, 0

    def link(self, ins):
        self.k += 1
        assert self.k <= self.per
        ins.then_inc(self.sem, 1)
        self.eng.wait_ge(self.sem, self.base + self.k)
        if self.apart is not None:
            self.eng.sem_inc(self.apart, 1)

    def end(self):
        assert self.k == self.per, (self.k, self.per)


def loop(eng, n, step, peel=1, unroll=1):
    for i in range(peel * unroll):
        step(i, i % unroll, i // unroll)
    with eng.Fori(peel, n // unroll - peel) as m:
        for r in range(unroll):
            step(m * unroll + r, r, m)
    for i in range(n - peel * unroll, n):
        step(i, i % unroll, i // unroll)


def flamingo_kernel(nc, x, ctx_in, mask, g_xattn, g_ffn,
                    w_q0, b_q0, w_kv0, b_kv0, w_o0, b_o0, w1_0, b1_0, w2_0, b2_0, wr0, br0,
                    w_q1, b_q1, w_k1, b_k1, w_v1, b_v1, wr1, br1, w1_1, b1_1, w2_1, b2_1, out):
    with ExitStack() as ctx:
        def sb(name, shape, dt=F32):
            return ctx.enter_context(nc.sbuf_tensor(name, shape, dt))

        def sem(name):
            return ctx.enter_context(nc.semaphore(name))

        slots_dram = nc.dram_tensor("slot_rows", (NSLOT, D), F32, kind="Internal").ap()
        yrows_dram = nc.dram_tensor("slot_outputs", (NSLOT, D), F32, kind="Internal").ap()

        xres = sb("xres", [P, NT, D])
        w1sb = sb("w1sb", [P, E * NC, 1024])
        w2sb = sb("w2sb", [P, E * 8, D])
        wq, wk, wv, wo = (sb(n, [P, NC, D]) for n in ("wq", "wk", "wv", "wo"))
        bq, bk = sb("bq", [P, NC]), sb("bk", [P, NC])
        bv = sb("bv", [Z, D])
        gated_bo = sb("gated_bo", [P, D])
        tg = sb("tg", [P, 4])
        ident = sb("ident", [P, P])
        headmask = {0: sb("headmask0", [P, 8]), 1: sb("headmask1", [P, 4])}
        maskneg = sb("maskneg", [P, TPB, Z])
        wr = sb("wr", [P, NC, E])
        brb = sb("brb", [P, E])
        gates = sb("gates", [P, NT])
        slot_f = sb("slot_f", [P, NT])
        slot_i = sb("slot_i", [P, NT], I32)
        tile_expert = sb("tile_expert", [1, 40], I32)
        expert_rows = sb("expert_rows", [96, E, P], BF16)
        biasw = sb("biasw", [96, 1024 + D], BF16)
        halfneg = sb("halfneg", [P, RG])
        eps = sb("eps", [P, RG])
        xs = [sb(f"xs{r}", [P, D]) for r in range(RING)]

        SCRATCH = 6560
        scratch = sb("scratch", [P, SCRATCH])

        def carve(*shapes):
            at, got = 0, []
            for shape in shapes:
                n = 1
                for s in shape[1:]:
                    n *= s
                ap = scratch[0:shape[0], at:at + n]
                if len(shape) == 3:
                    ap = ap.rearrange("p (a b) -> p a b", a=shape[1])
                got.append(ap)
                at += n
            assert at <= SCRATCH, at
            return got

        (xhat, xT, ctxs, cT, qT, kbd, vaug, p0, p1, pt0, pt1, attn, attnT, rawmask, xst, mv, veps, rstd, mx, rinv
         ) = carve([P, TPB, D], [P, NC, S], [Z, D], [P, NC, Z], [P, NC, S], [P, NC, 8 * Z], [Z, 16 * 17],
                   [P, 2, GZ], [P, 2, GZ], [Z, HG, P], [Z, HG, P], [P, D], [P, NC, P], [P, TPB, Z],
                   [P, TPB, 6], [P, TPB, 2], [P, TPB], [P, TPB], [P, 2 * HG], [P, 16])
        p_sb, pt_sb = [p0, p1], [pt0, pt1]
        (r_x, r_xT, logits, r_st, r_mv, r_veps, r_rstd, one_hot, work_a, work_b, tmax, tmax2, small
         ) = carve([P, RG, D], [P, RG * NC, P], [P, NT, E], [P, RG, 6], [P, RG, 2], [P, RG], [P, RG],
                   [P, NT, E], [P, NT * E], [P, NT * E], [P, NT], [P, NT], [P, 12, E])
        one_hot_b = sb("one_hot_b", [P, NT * E], BF16)
        upper = sb("upper", [P, P], BF16)
        ones_b = sb("ones_b", [P, P], BF16)
        exp_rev = sb("exp_rev", [P, E])
        steps128 = sb("steps128", [P, NT])
        tile_no = sb("tile_no", [1, 40, E])
        (f_xn, f_xT, f_h, f_hT, f_y0, f_y1, f_y2, f_st, f_mv, f_veps, f_rstd
         ) = carve([P, D], [P, NC, P], [P, 1024], [P, 8, P], [P, D], [P, D], [P, D], [P, 6], [P, 2], [P, 1], [P, 1])
        f_y = [f_y0, f_y1, f_y2]
        te_cmp, te_sum = carve([1, 40, E], [1, 40])[0:2]
        last_y = carve(*[[P, D]] * RG)
        biasf = {0: w1sb[0:96, 14:16, :].rearrange("p a b -> p (a b)"), 1: w1sb[0:96, 0, 256:768]}

        ps = ctx.enter_context(nc.psum_tensor("ps", [P, 8, 512], F32))

        const_loaded = {0: sem("const_loaded0"), 1: sem("const_loaded1")}
        const_made, const_chain, tanh_done, tgb_done = sem("const_made"), sem("const_chain"), sem("tanh_done"), sem("tgb_done")
        zero_stored, weights_loaded = sem("zero_stored"), {0: sem("weights_loaded0"), 1: sem("weights_loaded1")}
        bias_loaded, bias_split = {0: sem("bias_loaded0"), 1: sem("bias_loaded1")}, {0: sem("bias_split0"), 1: sem("bias_split1")}
        A = {}
        for L in (0, 1):
            for n in ("x_loaded", "ctx_loaded", "mask_loaded", "stats_done", "rstd_chain", "rstd_done", "xhat_done",
                      "prep_chain", "sm_chain", "xT_ps", "xT_sb", "cT_ps", "cT_sb", "q_ps", "q_sb", "kv_ps", "kbd_done",
                      "v_done", "s_ps", "sub_done", "exp_done", "pt_ps", "pt_sb", "av_ps", "attn_done", "at_ps", "at_sb",
                      "wo_ps", "res_done", "bo_done", "gathered0", "gathered1"):
                if L == 0 and n.startswith(("mask", "gath")) or L == 1 and n in ("x_loaded", "at_ps", "at_sb", "wo_ps", "bo_done"):
                    continue
                A[n, L] = sem(f"a{L}_{n}")
        R = {(n, L): sem(f"r{L}_{n}") for L in (0, 1) for n in (
            "stats_done", "chain", "rstd_chain", "rstd_done", "x_done", "xT_ps", "xT_sb", "lg_ps", "lg_done", "onehot_done",
            "rank_ps", "gate_exp", "route_chain", "routed", "scattered", "sub_done")}
        F = {(n, L): sem(f"f{L}_{n}") for L in (0, 1) for n in (
            ["chain", "stats_done", "rstd_chain", "rstd_done", "x_done", "xT_ps", "xT_sb", "h_ps", "h_sb", "hT_ps", "hT_sb",
             "y_ps", "y_sb"] + [f"xs_loaded{r}" for r in range(RING)] + [f"y_stored{r}" for r in range(RING)])}
        last_gathered = [sem(f"last_gathered{r}") for r in range(RG)]
        bias_zeroed = {0: sem("bias_zeroed0"), 1: sem("bias_zeroed1")}
        bias_link = {0: sem("bias_link0"), 1: sem("bias_link1")}
        vaug_ones = {0: sem("vaug_ones0"), 1: sem("vaug_ones1")}
        bq_done = sem("bq_done")
        wait_carried = sem("wait_carried")
        last_added, out_stored = sem("last_added"), sem("out_stored")

        n_const = {0: 12, 1: 8}

        block = ctx.enter_context(nc.Block())

        @block.sync
        def _(sp):
            def rows(w):
                return w.rearrange("(c p) n -> p c n", p=P)

            def cols(b):
                return b.rearrange("(c p) -> p c", p=P)

            def load_batch(L, b):
                if L == 0:
                    wait(sp, A["x_loaded", L], 16 * b)
                    sp.dma_start(xres[:, bass.ds(TPB * b, TPB), :],
                                 x[bass.ds(b, 1), :, :].rearrange("a (j p) d -> p (a j) d", p=P)).then_inc(A["x_loaded", L], 16)
                wait(sp, A["cT_ps", L], b)
                sp.dma_start(ctxs, ctx_in[bass.ds(b, 1), :, :].rearrange("a z d -> (a z) d")).then_inc(A["ctx_loaded", L], 16)
                if L == 1:
                    wait(sp, A["xhat_done", L], b)
                    sp.dma_start(rawmask, mask[bass.ds(b, 1), :, :].rearrange("a (j p) z -> p (a j) z", p=P)
                                 ).then_inc(A["mask_loaded", L], 16)

            def load_consts(L):
                q = const_loaded[L]
                pairs = [(wq, w_q0), (wk, w_kv0[:, 0:D]), (wv, w_kv0[:, D:2 * D]), (wo, w_o0)] if L == 0 else \
                        [(wq, w_q1), (wk, w_k1), (wv, w_v1)]
                for dst, src in pairs:
                    sp.dma_start(dst[:], rows(src)).then_inc(q, 16)
                for dst, src in ((bq, b_q0 if L == 0 else b_q1), (bk, b_kv0[0:D] if L == 0 else b_k1)):
                    sp.dma_start(dst[:], cols(src), allow_slow_non_contiguous=True).then_inc(q, 16)
                bsrc = b_kv0[D:2 * D] if L == 0 else b_v1
                sp.dma_start(bv[:], bsrc.partition_broadcast(Z)).then_inc(q, 16)
                sp.dma_start(wr[:], rows(wr0 if L == 0 else wr1)).then_inc(q, 16)
                sp.dma_start(brb[:], (br0 if L == 0 else br1).partition_broadcast(P)).then_inc(q, 16)
                if L == 0:
                    sp.dma_start(gated_bo[:], b_o0.partition_broadcast(P)).then_inc(q, 16)
                    sp.dma_start(tg[:, 0:2], g_xattn.partition_broadcast(P)).then_inc(q, 16)
                    sp.dma_start(tg[:, 2:4], g_ffn.partition_broadcast(P)).then_inc(q, 16)

            def load_biases(L):
                b1, b2 = (b1_0, b2_0) if L == 0 else (b1_1, b2_1)
                I = FFN[L]["I"]
                sp.wait_ge(bias_zeroed[L], 1)
                for q in range(3):
                    sp.dma_start(biasf[L][32 * q:32 * q + E, 0:I], b1).then_inc(bias_loaded[L], 16)
                    sp.dma_start(biasf[L][32 * q:32 * q + E, I:I + D], b2).then_inc(bias_loaded[L], 16)

            def load_weights(L, b):
                wait(sp, weights_loaded[L], 32 * b)
                if L == 0:
                    sp.dma_start(w1sb[:, bass.ds(b, 1), :],
                                 w1_0.rearrange("e (c p) n -> (e c) p n", p=P)[bass.ds(b, 1), :, :].rearrange("a p n -> p a n")
                                 ).then_inc(weights_loaded[L], 16)
                    sp.dma_start(w2sb[:, bass.ds(4 * b, 4), :],
                                 w2_0.rearrange("e (c p) n -> (e c) p n", p=P)[bass.ds(4 * b, 4), :, :].rearrange("a p n -> p a n")
                                 ).then_inc(weights_loaded[L], 16)
                else:
                    for dst, src in ((w1sb[:, :, 0:D], w1_1), (w2sb, w2_1)):
                        sp.dma_start(dst[:, bass.ds(b, 1), :],
                                     src.rearrange("e (c p) n -> (e c) p n", p=P)[bass.ds(b, 1), :, :].rearrange("a p n -> p a n")
                                     ).then_inc(weights_loaded[L], 16)

            def experts_io(L):
                sp.wait_ge(zero_stored, 16)
                sp.wait_ge(R["scattered", L], 16 * NT)

                def load(i, r):
                    sp.dma_start(xs[r][:], slots_dram[bass.ds(i * P, P), :]).then_inc(F["xs_loaded%d" % r, L], 16)

                for i in range(RING):
                    load(i, i)

                def step(i, r, m):
                    if not isinstance(i, int) or i + RING < SLOT_TILES:
                        sp.wait_ge(F["x_done", L], i + 1)
                        sp.dma_start(xs[r][:], slots_dram[bass.ds((i + RING) * P, P), :]).then_inc(F["xs_loaded%d" % r, L], 16)
                    sp.wait_ge(F["y_sb", L], i + 1)
                    sp.dma_start(yrows_dram[bass.ds(i * P, P), :], f_y[r]).then_inc(F["y_stored%d" % r, L], 16)

                loop(sp, SLOT_TILES, step, unroll=RING)

            for L in (0, 1):
                if L == 1:
                    sp.wait_ge(R["scattered", 0], 16 * NT)
                if L == 0:
                    load_batch(0, 0)
                load_consts(L)
                if L == 1:
                    load_biases(1)
                    for r in range(RING):
                        sp.wait_ge(F["y_stored%d" % r, 0], 16 * (SLOT_TILES // RING))
                    load_batch(1, 0)
                else:
                    load_biases(0)
                if L == 1:
                    sp.wait_ge(bias_split[1], 1)
                load_weights(L, 0)
                with sp.Fori(1, 14) as b:
                    load_batch(L, b)
                    load_weights(L, b)
                sp.wait_ge(bias_split[L], 1)
                for b in (14, 15):
                    load_batch(L, b)
                    load_weights(L, b)
                experts_io(L)

            with sp.Fori(0, NT // RG) as m:
                sp.wait_ge(last_added, RG * m + RG)
                sp.dma_start(out.rearrange("b (j p) d -> p (b j) d", p=P)[:, bass.ds(RG * m, RG), :],
                             xres[:, bass.ds(RG * m, RG), :]).then_inc(out_stored, 16)
            sp.wait_ge(out_stored, 16 * (NT // RG))

        @block.gpsimd
        def _(pool):
            c = [0]

            def link(ins):
                c[0] += 1
                ins.then_inc(const_chain, 1)
                pool.wait_ge(const_chain, c[0])

            pool.memset(xs[0][:], 0.0).then_inc(const_made, 1)
            for t in (ident, expert_rows, maskneg):
                pool.memset(t[:], 0.0)
            for t in (headmask[0], headmask[1], upper, ones_b):
                pool.memset(t[:], 1.0)
            pool.memset(eps[:], EPS)
            link(pool.memset(halfneg[:], -0.5))
            pool.affine_select(ident[:], ident[:], pattern=[[-1, P]], compare_op=ALU.not_equal, fill=1.0, base=0,
                               channel_multiplier=1)
            for L in (0, 1):
                n, d = ATT[L]["hpc"], P // ATT[L]["hpc"]
                link(pool.affine_select(headmask[L][:], headmask[L][:], pattern=[[-d, n]], compare_op=ALU.is_ge,
                                        fill=0.0, base=0, channel_multiplier=1))
                link(pool.affine_select(headmask[L][:], headmask[L][:], pattern=[[d, n]], compare_op=ALU.is_ge,
                                        fill=0.0, base=d - 1, channel_multiplier=-1))
            pool.affine_select(maskneg[:, 0, :], maskneg[:, 0, :], pattern=[[-1, Z]], compare_op=ALU.is_gt,
                               fill=-ATT[0]["mask_val"], base=0, channel_multiplier=1).then_inc(const_made, 1)
            for q in range(3):
                link(pool.affine_select(expert_rows[:], expert_rows[:], pattern=[[-1, E], [0, P]],
                                        compare_op=ALU.not_equal, fill=1.0, base=-32 * q, channel_multiplier=1))
            pool.affine_select(upper[:], upper[:], pattern=[[1, P]], compare_op=ALU.is_gt, fill=0.0, base=0,
                               channel_multiplier=-1)
            pool.iota(exp_rev[:], pattern=[[-1, E]], base=E, channel_multiplier=0, allow_small_or_imprecise_dtypes=True)
            pool.iota(steps128[:], pattern=[[P, NT]], base=0, channel_multiplier=0, allow_small_or_imprecise_dtypes=True)
            pool.iota(tile_no[:], pattern=[[1, 40], [0, E]], base=0, channel_multiplier=0,
                      allow_small_or_imprecise_dtypes=True).then_inc(const_made, 1)
            pool.wait_ge(tanh_done, 1)
            pool.tensor_scalar(gated_bo[:], gated_bo[:], tg[:, 0:1], None, ALU.mult).then_inc(tgb_done, 1)

            def make_rstd(stats_done, chain, done, step, var, plus_eps, rs, n):
                pool.wait_ge(stats_done, step + 1)
                pool.tensor_tensor(plus_eps, var, eps[:, 0:n], ALU.add).then_inc(chain, 1)
                pool.wait_ge(chain, step + 1)
                pool.tensor_tensor(rs, plus_eps, halfneg[:, 0:n], ALU.pow).then_inc(done, 1)

            for L in (0, 1):
                def rstd_batch(b):
                    make_rstd(A["stats_done", L], A["rstd_chain", L], A["rstd_done", L], b, mv[:, :, 1], veps, rstd, TPB)

                if L == 0:
                    pool.wait_ge(tgb_done, 1)
                    rstd_batch(0)

                    def batch0(b, _r, _m):
                        if not isinstance(b, int) or b + 1 < NB:
                            rstd_batch(b + 1)
                        for j in range(TPB):
                            pool.wait_ge(A["res_done", 0], TPB * b + j + 1)
                            t = xres[:, bass.ds(TPB * b + j, 1), :].rearrange("p a d -> p (a d)")
                            pool.tensor_tensor(t, t, gated_bo[:], ALU.add).then_inc(A["bo_done", 0], 1)

                    loop(pool, NB, batch0)
                else:
                    for r in range(RING):
                        pool.wait_ge(F["y_stored%d" % r, 0], 16 * (SLOT_TILES // RING))
                    for b in range(NB):
                        wait(pool, A["stats_done", 1], b)
                        for j in range(TPB):
                            t = TPB * b + j
                            pool.indirect_dma_start(xs[j][:], None, yrows_dram,
                                                    bass.IndirectOffsetOnAxis(ap=slot_i[:, t:t + 1], axis=0)
                                                    ).then_inc(A["gathered%d" % j, 1], 16)
                        rstd_batch(b)

                with pool.Fori(0, NT // RG) as g:
                    make_rstd(R["stats_done", L], R["rstd_chain", L], R["rstd_done", L], g, r_mv[:, :, 1], r_veps, r_rstd, RG)
                pool.wait_ge(R["routed", L], 1)
                if L == 0:
                    pool.wait_ge(zero_stored, 16)
                for t in range(NT):
                    pool.indirect_dma_start(slots_dram, bass.IndirectOffsetOnAxis(ap=slot_i[:, t:t + 1], axis=0),
                                            xres[:, t, :], None).then_inc(R["scattered", L], 16)
                with pool.Fori(0, SLOT_TILES) as i:
                    make_rstd(F["stats_done", L], F["rstd_chain", L], F["rstd_done", L], i, f_mv[:, 1:2], f_veps, f_rstd, 1)

            for r in range(RING):
                pool.wait_ge(F["y_stored%d" % r, 1], 16 * (SLOT_TILES // RING))
            for t in range(NT):
                wait(pool, last_added, t - RG + 1)
                pool.indirect_dma_start(last_y[t % RG], None, yrows_dram,
                                        bass.IndirectOffsetOnAxis(ap=slot_i[:, t:t + 1], axis=0)
                                        ).then_inc(last_gathered[t % RG], 16)

        @block.scalar
        def _(act):
            act.wait_ge(const_made, 1)
            act.dma_start(slots_dram.rearrange("(n p) d -> p n d", p=P),
                          xs[0][:].unsqueeze(1).broadcast_to([P, SLOT_TILES, D])).then_inc(zero_stored, 16)
            act.wait_ge(const_loaded[0], 16 * n_const[0])
            act.activation(tg[:], tg[:], ACT.Tanh).then_inc(tanh_done, 1)

            for L in (0, 1):
                U = ATT[L]["units"]
                if L == 1:
                    act.wait_ge(const_loaded[1], 16 * n_const[1])
                    act.activation(bq[:], bq[:], ACT.Copy, scale=(D // ATT[1]["H"]) ** -0.5).then_inc(bq_done, 1)
                    act.wait_ge(bq_done, 1)

                def xT_evac(b):
                    act.wait_ge(A["xT_ps", L], b + 1)
                    wait(act, A["q_ps", L], b)
                    act.activation(xT.rearrange("p a b -> p (a b)"), ps[:, 7, :], ACT.Copy).then_inc(A["xT_sb", L], 1)

                def cT_evac(b):
                    act.wait_ge(A["cT_ps", L], b + 1)
                    wait(act, A["kv_ps", L], b)
                    act.activation(cT.rearrange("p a b -> p (a b)"), ps[:, 7, 0:NC * Z], ACT.Copy).then_inc(A["cT_sb", L], 1)

                def q_evac(b):
                    act.wait_ge(A["q_ps", L], b + 1)
                    wait(act, A["s_ps", L], U * b)
                    for f in range(NC):
                        ins = act.activation(qT[:, f, :], ps[:, 7, f * S:(f + 1) * S], ACT.Identity, bias=bq[:, f:f + 1],
                                             scale=1.0 if L == 0 else (D // ATT[1]["H"]) ** -0.5)
                    ins.then_inc(A["q_sb", L], 1)

                def exp_unit(b, u):
                    n = U * b + u
                    act.wait_ge(A["sub_done", L], n + 1)
                    act.activation(p_sb[u % 2], p_sb[u % 2], ACT.Exp).then_inc(A["exp_done", L], 1)

                def pt_evac(b, u):
                    n = U * b + u
                    for g in range(2):
                        act.wait_ge(A["pt_ps", L], 2 * n + g + 1)
                        if g == 0:
                            wait(act, A["av_ps", L], n)
                        act.activation(pt_sb[g].rearrange("p a b -> p (a b)"), ps[0:Z, 4 + g, :], ACT.Copy
                                       ).then_inc(A["pt_sb", L], 1)

                def attnT_evac(b, j):
                    act.wait_ge(A["at_ps", L], TPB * b + j + 1)
                    wait(act, A["wo_ps", L], TPB * b + j)
                    act.activation(attnT.rearrange("p a b -> p (a b)"), ps[:, 6, 0:D], ACT.Copy).then_inc(A["at_sb", L], 1)

                xT_evac(0)
                cT_evac(0)
                q_evac(0)

                def batch(b, _r, _m):
                    nxt = not isinstance(b, int) or b + 1 < NB
                    exp_unit(b, 0)
                    pt_evac(b, 0)
                    exp_unit(b, 1)
                    pt_evac(b, 1)
                    if nxt:
                        xT_evac(b + 1)
                    if L == 0:
                        exp_unit(b, 2)
                        if nxt:
                            cT_evac(b + 1)
                        pt_evac(b, 2)
                        if nxt:
                            q_evac(b + 1)
                        attnT_evac(b, 0)
                        exp_unit(b, 3)
                        pt_evac(b, 3)
                        attnT_evac(b, 1)
                    elif nxt:
                        cT_evac(b + 1)
                        q_evac(b + 1)

                loop(act, NB, batch)

                with act.Fori(0, NT // RG) as g:
                    act.wait_ge(R["xT_ps", L], g + 1)
                    act.activation(r_xT.rearrange("p (h a) b -> p h (a b)", h=2), ps[:, 0:2, :], ACT.Copy).then_inc(R["xT_sb", L], 1)
                if L == 0:
                    act.wait_ge(R["sub_done", 0], 1)
                    act.activation(gates[:], gates[:], ACT.Exp).then_inc(R["gate_exp", 0], 1)

                I, CW = FFN[L]["I"], FFN[L]["CW"]
                NCH = I // CW

                def gelu(i, n):
                    act.wait_ge(F["h_ps", L], NCH * i + n + 1)
                    wait(act, F["hT_ps", L], NCH * (i - 1) + n + 1)
                    act.activation(f_h[:, n * CW:(n + 1) * CW], ps[:, n, 0:CW], ACT.Gelu).then_inc(F["h_sb", L], 1)

                for n in range(NCH):
                    gelu(0, n)

                def tile(i, r, m):
                    if not isinstance(i, int) or i + 1 < SLOT_TILES:
                        for n in range(NCH):
                            gelu(i + 1, n)
                    act.wait_ge(F["y_ps", L], i + 1)
                    wait(act, F["y_stored%d" % r, L], 16 * m)
                    act.activation(f_y[r], ps[:, 6, 0:D], ACT.Copy).then_inc(F["y_sb", L], 1)

                loop(act, SLOT_TILES, tile, unroll=RING)

        @block.tensor
        def _(pe):
            pe.wait_ge(const_made, 3)
            for L in (0, 1):
                U, H, hpc = (ATT[L][k] for k in ("units", "H", "hpc"))
                d = D // H
                pe.wait_ge(const_loaded[L], 16 * n_const[L])

                def turn_x(b):
                    pe.wait_ge(A["xhat_done", L], b + 1)
                    wait(pe, A["v_done", L], b)
                    for c in range(NC):
                        for j in range(TPB):
                            ins = pe.transpose(ps[:, 7, c * S + j * P:c * S + (j + 1) * P], xhat[:, j, c * P:(c + 1) * P], ident[:])
                    ins.then_inc(A["xT_ps", L], 1)

                def turn_ctx(b):
                    pe.wait_ge(A["ctx_loaded", L], 16 * b + 16)
                    pe.wait_ge(A["xT_sb", L], b + 1)
                    for c in range(NC):
                        ins = pe.transpose(ps[:, 7, c * Z:(c + 1) * Z], ctxs[:, c * P:(c + 1) * P], ident[0:Z, 0:Z])
                    ins.then_inc(A["cT_ps", L], 1)

                def project_q(b):
                    pe.wait_ge(A["cT_sb", L], b + 1)
                    for f in range(NC):
                        for k in range(NC):
                            ins = pe.matmul(ps[:, 7, f * S:(f + 1) * S], wq[:, k, f * P:(f + 1) * P], xT[:, k, :],
                                            start=(k == 0), stop=(k == NC - 1))
                    ins.then_inc(A["q_ps", L], 1)

                def project_kv(b):
                    pe.wait_ge(A["q_sb", L], b + 1)
                    for f in range(NC):
                        for k in range(NC):
                            pe.matmul(ps[:, 7, f * Z:(f + 1) * Z], wk[:, k, f * P:(f + 1) * P], cT[:, k, :],
                                      start=(k == 0), stop=(k == NC - 1))
                    for k in range(NC):
                        ins = pe.matmul(ps[0:Z, 7, D:2 * D], cT[:, k, :], wv[:, k, :], start=(k == 0), stop=(k == NC - 1))
                    ins.then_inc(A["kv_ps", L], 1)

                def scores(b, u):
                    n, buf = U * b + u, u % 2
                    if u == 0:
                        pe.wait_ge(A["kbd_done", L], b + 1)
                        pe.wait_ge(A["q_sb", L], b + 1)
                    wait(pe, A["sub_done", L], n - 1)
                    for g in range(2):
                        if L == 0:
                            lhs, rhs = qT[:, u % 2, (u // 2) * P:(u // 2 + 1) * P], kbd[:, u % 2, g * GZ:(g + 1) * GZ]
                        else:
                            lhs, rhs = qT[:, g, u * P:(u + 1) * P], kbd[:, g, 0:GZ]
                        ins = pe.matmul(ps[:, 2 * buf + g, 0:GZ], lhs, rhs, start=True, stop=True)
                    ins.then_inc(A["s_ps", L], 1)

                def turn_p(b, u):
                    n = U * b + u
                    pe.wait_ge(A["exp_done", L], n + 1)
                    for g in range(2):
                        wait(pe, A["pt_sb", L], 2 * n + g - 1)
                        for k in range(HG):
                            ins = pe.transpose(ps[0:Z, 4 + g, k * P:(k + 1) * P], p_sb[u % 2][:, g, k * Z:(k + 1) * Z], ident[:])
                        ins.then_inc(A["pt_ps", L], 1)

                def weigh_v(b, u):
                    n = U * b + u
                    j, first = (u // 2, u % 2 == 0) if L == 0 else (u, True)
                    if u == 0:
                        pe.wait_ge(A["v_done", L], b + 1)
                    if first:
                        wait(pe, A["res_done" if L == 0 else "attn_done", L], TPB * b + j)
                    for g in range(2):
                        pe.wait_ge(A["pt_sb", L], 2 * n + g + 1)
                        for k in range(HG):
                            h = (u % 2) * 8 + g * HG + k if L == 0 else g * HG + k
                            ins = pe.matmul(ps[:, 6, h * (d + 1):(h + 1) * (d + 1)], pt_sb[g][:, k, :],
                                            vaug[:, h * (d + 1):(h + 1) * (d + 1)], start=True, stop=True)
                    ins.then_inc(A["av_ps", L], 1)

                def turn_attn(b, j):
                    pe.wait_ge(A["attn_done", L], TPB * b + j + 1)
                    for c in range(NC):
                        ins = pe.transpose(ps[:, 6, c * P:(c + 1) * P], attn[:, c * P:(c + 1) * P], ident[:])
                    ins.then_inc(A["at_ps", L], 1)

                def project_out(b, j):
                    pe.wait_ge(A["at_sb", L], TPB * b + j + 1)
                    for k in range(NC):
                        ins = pe.matmul(ps[:, 6, 0:D], attnT[:, k, :], wo[:, k, :], start=(k == 0), stop=(k == NC - 1))
                    ins.then_inc(A["wo_ps", L], 1)

                turn_x(0)
                turn_ctx(0)
                project_q(0)
                project_kv(0)
                scores(0, 0)

                def batch(b, _r, _m):
                    nxt = not isinstance(b, int) or b + 1 < NB
                    scores(b, 1)
                    turn_p(b, 0)
                    if L == 0:
                        scores(b, 2)
                    weigh_v(b, 0)
                    turn_p(b, 1)
                    if nxt:
                        turn_x(b + 1)
                    if L == 0:
                        scores(b, 3)
                        weigh_v(b, 1)
                        if nxt:
                            turn_ctx(b + 1)
                        turn_p(b, 2)
                        if nxt:
                            project_q(b + 1)
                        turn_attn(b, 0)
                        if nxt:
                            project_kv(b + 1)
                        project_out(b, 0)
                        weigh_v(b, 2)
                        turn_p(b, 3)
                        if nxt:
                            scores(b + 1, 0)
                        weigh_v(b, 3)
                        turn_attn(b, 1)
                        project_out(b, 1)
                    else:
                        if nxt:
                            turn_ctx(b + 1)
                            project_q(b + 1)
                            project_kv(b + 1)
                        weigh_v(b, 1)
                        if nxt:
                            scores(b + 1, 0)

                loop(pe, NB, batch)

                def r_turn(g):
                    pe.wait_ge(R["x_done", L], g + 1)
                    wait(pe, R["xT_sb", L], g)
                    for q in range(RG):
                        for c in range(NC):
                            m = q * NC + c
                            ins = pe.transpose(ps[:, m // 4, (m % 4) * P:(m % 4 + 1) * P], r_x[:, q, c * P:(c + 1) * P], ident[:])
                    ins.then_inc(R["xT_ps", L], 1)

                def r_logits(g):
                    pe.wait_ge(R["xT_sb", L], g + 1)
                    wait(pe, R["lg_done", L], g)
                    for q in range(RG):
                        for c in range(NC):
                            ins = pe.matmul(ps[:, 2, q * E:(q + 1) * E], r_xT[:, q * NC + c, :], wr[:, c, :],
                                            start=(c == 0), stop=(c == NC - 1))
                    ins.then_inc(R["lg_ps", L], 1)

                def r_step(g, _r, _m):
                    r_turn(g)
                    r_logits(g)

                loop(pe, NT // RG, r_step)
                pe.wait_ge(R["onehot_done", L], 1)
                pe.matmul(ps[:, 3, 0:NT * E], upper[:], one_hot_b[:], start=True, stop=True)
                pe.matmul(ps[:, 3, NT * E:2 * NT * E], ones_b[:], one_hot_b[:], start=True, stop=True
                          ).then_inc(R["rank_ps", L], 1)

                I, CW = FFN[L]["I"], FFN[L]["CW"]
                NCH, KC = I // CW, I // P
                pe.wait_ge(weights_loaded[L], 16 * 2 * NB)
                pe.wait_ge(bias_split[L], 1)
                pe.wait_ge(R["routed", L], 1)

                def f_turn(i):
                    pe.wait_ge(F["x_done", L], i + 1)
                    wait(pe, F["xT_sb", L], i)
                    for c in range(NC):
                        ins = pe.transpose(ps[:, 5, c * P:(c + 1) * P], f_xn[:, c * P:(c + 1) * P], ident[:])
                    ins.then_inc(F["xT_ps", L], 1)

                def expert_of(i):
                    return pe.value_load(tile_expert[0:1, bass.ds(i, 1)], min_val=0, max_val=E - 1)

                def flat(ap):
                    return ap.rearrange("p a b -> p (a b)")

                def hidden(i, n, e):
                    if n == 0:
                        pe.wait_ge(F["xT_sb", L], i + 1)
                    wait(pe, F["h_sb", L], NCH * (i - 1) + n + 1)
                    pe.matmul(ps[:, n, 0:CW], flat(expert_rows[:, bass.ds(e, 1), :]), biasw[:, n * CW:(n + 1) * CW],
                              start=True, stop=False)
                    for k in range(NC):
                        ins = pe.matmul(ps[:, n, 0:CW], f_xT[:, k, :], flat(w1sb[:, bass.ds(e * NC + k, 1), n * CW:(n + 1) * CW]),
                                        start=False, stop=(k == NC - 1))
                    ins.then_inc(F["h_ps", L], 1)

                def turn_h(i, n):
                    pe.wait_ge(F["h_sb", L], NCH * i + n + 1)
                    wait(pe, F["hT_sb", L], NCH * (i - 1) + n + 1)
                    for q in range(CW // P):
                        ins = pe.transpose(ps[:, 2 + n, q * P:(q + 1) * P], f_h[:, n * CW + q * P:n * CW + (q + 1) * P], ident[:])
                    ins.then_inc(F["hT_ps", L], 1)

                def down(i, e):
                    wait(pe, F["y_sb", L], i)
                    pe.matmul(ps[:, 6, 0:D], flat(expert_rows[:, bass.ds(e, 1), :]), biasw[:, I:I + D], start=True, stop=False)
                    for k in range(KC):
                        if k % (CW // P) == 0:
                            pe.wait_ge(F["hT_sb", L], NCH * i + k // (CW // P) + 1)
                        ins = pe.matmul(ps[:, 6, 0:D], f_hT[:, k, :], flat(w2sb[:, bass.ds(e * KC + k, 1), :]),
                                        start=False, stop=(k == KC - 1))
                    ins.then_inc(F["y_ps", L], 1)

                f_turn(0)
                e0 = expert_of(0)
                for n in range(NCH):
                    hidden(0, n, e0)

                def tile(i, _r, _m):
                    nxt = not isinstance(i, int) or i + 1 < SLOT_TILES
                    if nxt:
                        f_turn(i + 1)
                        e_next = expert_of(i + 1)
                        if NCH == 2:
                            hidden(i + 1, 0, e_next)
                    for n in range(NCH):
                        turn_h(i, n)
                    if nxt:
                        hidden(i + 1, NCH - 1, e_next)
                    down(i, expert_of(i))

                loop(pe, SLOT_TILES, tile)

        @block.vector
        def _(dve):
            def split_bias(L):
                n = FFN[L]["I"] + D
                f = biasf[L][:, 0:n]
                dve.wait_ge(bias_loaded[L], 16 * 6)
                w = biasw[:, 0:n]
                bl = bias_link[L]
                k = [0]

                def link(ins):
                    k[0] += 1
                    ins.then_inc(bl, 1)
                    dve.wait_ge(bl, k[0])

                link(dve.tensor_copy(w, f))
                link(dve.tensor_tensor(f, f, w, ALU.subtract))
                dve.tensor_copy(w[32:64], f[32:64])
                link(dve.tensor_copy(w[64:96], f[64:96]))
                link(dve.tensor_tensor(f[64:96], f[64:96], w[64:96], ALU.subtract))
                dve.tensor_copy(w[64:96], f[64:96]).then_inc(bias_split[L], 1)

            dve.memset(biasf[0][:, 0:FFN[0]["I"] + D], 0.0).then_inc(bias_zeroed[0], 1)
            for L in (0, 1):
                U, H, hpc = (ATT[L][k] for k in ("units", "H", "hpc"))
                d = D // H
                prep = Chain(dve, A["prep_chain", L], 1 if L == 0 else 2, wait_carried)
                att = Chain(dve, A["sm_chain", L], 8 if L == 0 else 6)
                hm = headmask[L]

                def row(t, n=1):
                    return xres[:, bass.ds(t, n), :].rearrange("p a d -> p (a d)")

                def prep_stats(b):
                    prep.begin(b)
                    if L == 0:
                        dve.wait_ge(A["x_loaded", 0], 16 * b + 16)
                    else:
                        for j in range(TPB):
                            t = TPB * b + j
                            dve.wait_ge(A["gathered%d" % j, 1], 16 * b + 16)
                            ins = dve.scalar_tensor_tensor(out=row(t), in0=xs[j][:], scalar=gates[:, bass.ds(t, 1)],
                                                           in1=row(t), op0=ALU.mult, op1=ALU.add)
                        prep.link(ins)
                    wait(dve, A["xhat_done", L], b)
                    dve.sem_inc(wait_carried, 1)
                    for j in range(TPB):
                        ins = dve.bn_stats(xst[:, j, :], row(TPB * b + j))
                    prep.link(ins)
                    for j in range(TPB):
                        ins = dve.bn_aggr(mv[:, j, :], xst[:, j, :])
                    ins.then_inc(A["stats_done", L], 1)
                    prep.end()

                def prep_apply(b):
                    if L == 1:
                        dve.wait_ge(A["mask_loaded", 1], 16 * b + 16)
                        dve.tensor_scalar(maskneg[:], rawmask, -ATT[1]["mask_val"], None, ALU.mult)
                    dve.wait_ge(A["rstd_done", L], b + 1)
                    wait(dve, A["xT_ps", L], b)
                    for j in range(TPB):
                        ins = dve.tensor_scalar(xhat[:, j, :], row(TPB * b + j), mv[:, j, 0:1], rstd[:, j:j + 1],
                                                ALU.subtract, ALU.mult)
                    ins.then_inc(A["xhat_done", L], 1)

                def make_kbd(b):
                    dve.wait_ge(A["kv_ps", L], b + 1)
                    wait(dve, A["s_ps", L], U * b)
                    for c in range(NC):
                        ins = dve.scalar_tensor_tensor(
                            out=kbd[:, c, 0:hpc * Z].rearrange("p (h z) -> p h z", h=hpc),
                            in0=ps[:, 7, c * Z:(c + 1) * Z].unsqueeze(1).broadcast_to([P, hpc, Z]), scalar=bk[:, c:c + 1],
                            in1=hm[:].unsqueeze(2).broadcast_to([P, hpc, Z]), op0=ALU.add, op1=ALU.mult)
                    ins.then_inc(A["kbd_done", L], 1)

                def make_v(b):
                    wait(dve, A["av_ps", L], U * b)
                    dve.tensor_tensor(vaug[:, 0:H * (d + 1)].rearrange("p (h e) -> p h e", h=H)[:, :, 0:d],
                                      ps[0:Z, 7, D:2 * D].rearrange("p (h e) -> p h e", h=H),
                                      bv[:].rearrange("p (h e) -> p h e", h=H), ALU.add).then_inc(A["v_done", L], 1)

                def softmax_unit(b, u):
                    n, buf = U * b + u, u % 2
                    dve.wait_ge(A["s_ps", L], n + 1)
                    wait(dve, A["pt_ps", L], 2 * (n - 1))
                    src = ps[:, 2 * buf:2 * buf + 2, 0:GZ].rearrange("p g (k z) -> p g k z", k=HG)
                    dst = p_sb[buf].rearrange("p g (k z) -> p g k z", k=HG)
                    j = u // 2 if L == 0 else u
                    if L == 1 or j == 0:
                        m = maskneg[:, j, :].unsqueeze(1).unsqueeze(1).broadcast_to([P, 2, HG, Z])
                        att.link(dve.tensor_tensor(dst, src, m, ALU.add))
                        src = dst
                    m8 = mx.rearrange("p (g k) -> p g k", g=2)
                    wait(dve, A["sub_done", L], n)
                    att.link(dve.tensor_reduce(m8, src, AX, ALU.max))
                    dve.tensor_tensor(dst, src, m8.unsqueeze(3).broadcast_to([P, 2, HG, Z]), ALU.subtract
                                      ).then_inc(A["sub_done", L], 1)

                def normalise(b, j):
                    dve.wait_ge(A["av_ps", L], U * b + (2 * j + 2 if L == 0 else j + 1))
                    av = ps[:, 6, 0:H * (d + 1)].rearrange("p (h e) -> p h e", h=H)
                    wait(dve, A["attn_done", L], TPB * b + j)
                    att.link(dve.reciprocal(rinv[:, 0:H].unsqueeze(2), av[:, :, d:d + 1]))
                    if L == 0:
                        wait(dve, A["at_ps", 0], TPB * b + j)
                    else:
                        wait(dve, A["res_done", 1], TPB * b + j)
                    ins = dve.tensor_tensor(attn.rearrange("p (h e) -> p h e", h=H), av[:, :, 0:d],
                                            rinv[:, 0:H].unsqueeze(2).broadcast_to([P, H, d]), ALU.mult)
                    ins.then_inc(A["attn_done", L], 1)
                    if L == 1:
                        dve.wait_ge(A["attn_done", 1], TPB * b + j + 1)
                        t = row(TPB * b + j)
                        dve.scalar_tensor_tensor(out=t, in0=attn, scalar=tg[:, 1:2], in1=t, op0=ALU.mult, op1=ALU.add
                                                 ).then_inc(A["res_done", 1], 1)

                def residual(b, j):
                    dve.wait_ge(A["wo_ps", L], TPB * b + j + 1)
                    t = row(TPB * b + j)
                    dve.scalar_tensor_tensor(out=t, in0=ps[:, 6, 0:D], scalar=tg[:, 0:1], in1=t, op0=ALU.mult, op1=ALU.add
                                             ).then_inc(A["res_done", L], 1)

                if L == 0:
                    dve.wait_ge(const_made, 3)
                    dve.wait_ge(tanh_done, 1)
                else:
                    for r in range(RING):
                        dve.wait_ge(F["y_stored%d" % r, 0], 16 * (SLOT_TILES // RING))
                    dve.wait_ge(const_loaded[1], 16 * n_const[1])
                    dve.memset(biasf[1], 0.0).then_inc(bias_zeroed[1], 1)
                dve.memset(vaug, 1.0).then_inc(vaug_ones[L], 1)
                dve.wait_ge(vaug_ones[L], 1)
                prep_stats(0)
                prep_apply(0)
                make_kbd(0)
                make_v(0)
                split_bias(L)

                def batch(b, _r, _m):
                    nxt = not isinstance(b, int) or b + 1 < NB
                    att.begin(b)
                    softmax_unit(b, 0)
                    if nxt:
                        prep_stats(b + 1)
                    softmax_unit(b, 1)
                    if nxt:
                        prep_apply(b + 1)
                    if L == 0:
                        softmax_unit(b, 2)
                        normalise(b, 0)
                        softmax_unit(b, 3)
                        if nxt:
                            make_kbd(b + 1)
                        residual(b, 0)
                        normalise(b, 1)
                        if nxt:
                            make_v(b + 1)
                        residual(b, 1)
                    else:
                        normalise(b, 0)
                        if nxt:
                            make_kbd(b + 1)
                        normalise(b, 1)
                        if nxt:
                            make_v(b + 1)
                    att.end()

                loop(dve, NB, batch)

                if L == 0:
                    dve.wait_ge(A["bo_done", 0], NT)
                dve.wait_ge(A["res_done", L], NT)
                rch = Chain(dve, R["chain", L], 1, wait_carried)

                def r_stats(g):
                    rch.begin(g)
                    wait(dve, R["x_done", L], g)
                    dve.sem_inc(wait_carried, 1)
                    for q in range(RG):
                        ins = dve.bn_stats(r_st[:, q, :], row(RG * g + q))
                    rch.link(ins)
                    for q in range(RG):
                        ins = dve.bn_aggr(r_mv[:, q, :], r_st[:, q, :])
                    ins.then_inc(R["stats_done", L], 1)

                def r_apply(g):
                    dve.wait_ge(R["rstd_done", L], g + 1)
                    wait(dve, R["xT_ps", L], g)
                    for q in range(RG):
                        ins = dve.tensor_scalar(r_x[:, q, :], row(RG * g + q), r_mv[:, q, 0:1], r_rstd[:, q:q + 1],
                                                ALU.subtract, ALU.mult)
                    ins.then_inc(R["x_done", L], 1)

                def r_logits(g):
                    dve.wait_ge(R["lg_ps", L], g + 1)
                    dve.tensor_tensor(logits[:, bass.ds(RG * g, RG), :], ps[:, 2, 0:RG * E].rearrange("p (q e) -> p q e", q=RG),
                                      brb[:].unsqueeze(1).broadcast_to([P, RG, E]), ALU.add).then_inc(R["lg_done", L], 1)

                r_stats(0)
                r_apply(0)

                def r_step(g, _r, _m):
                    if not isinstance(g, int) or g + 1 < NT // RG:
                        r_stats(g + 1)
                        r_apply(g + 1)
                    r_logits(g)

                loop(dve, NT // RG, r_step)

                ch = Chain(dve, R["route_chain", L], 1000)
                ch.begin(0)
                link = ch.link
                dve.wait_ge(R["lg_done", L], NT // RG)

                def te(ap):
                    return ap.rearrange("p (e t) -> p t e", e=E)

                def over_e(ap):
                    return ap.unsqueeze(2).broadcast_to([P, NT, E])

                wa, wb = work_a.rearrange("p (t e) -> p t e", e=E), work_b.rearrange("p (t e) -> p t e", e=E)
                link(dve.tensor_reduce(tmax, logits, AX, ALU.max))
                link(dve.tensor_tensor(wa, logits, over_e(tmax), ALU.is_equal))
                link(dve.tensor_tensor(wa, wa, exp_rev[:].unsqueeze(1).broadcast_to([P, NT, E]), ALU.mult))
                link(dve.tensor_reduce(tmax2, wa, AX, ALU.max))
                link(dve.tensor_tensor(one_hot, wa, over_e(tmax2), ALU.is_equal))
                dve.tensor_copy(te(one_hot_b[:]), one_hot).then_inc(R["onehot_done", L], 1)
                if L == 0:
                    link(dve.scalar_tensor_tensor(out=wb, in0=one_hot, scalar=-3.0e38, in1=logits, op0=ALU.mult, op1=ALU.add))
                    link(dve.tensor_reduce(tmax2, wb, AX, ALU.max))
                    dve.tensor_tensor(gates[:], tmax2, tmax, ALU.subtract).then_inc(R["sub_done", 0], 1)
                    dve.wait_ge(R["gate_exp", 0], 1)
                    link(dve.tensor_scalar(gates[:], gates[:], 1.0, None, ALU.add))
                    link(dve.reciprocal(gates[:], gates[:]))
                    link(dve.tensor_scalar(gates[:], gates[:], tg[:, 2:3], None, ALU.mult))
                else:
                    link(dve.memset(gates[:], 1.0))
                    link(dve.tensor_scalar(gates[:], gates[:], tg[:, 3:4], None, ALU.mult))
                link(dve.memset(work_a, 1.0))
                dve.wait_ge(R["rank_ps", L], 1)
                in_tile, of_tile = ps[:, 3, 0:NT * E], ps[:, 3, NT * E:2 * NT * E]
                cend, cstart, total, tiles, tend, ones8, tbase, off = (small[:, q, :] for q in range(8))
                link(dve.tensor_tensor_scan(work_b, work_a, of_tile, 0.0, ALU.mult, ALU.add))
                link(dve.memset(small.rearrange("p a b -> p (a b)"), 0.0))
                link(dve.tensor_copy(cend, work_b.rearrange("p (e t) -> p e t", e=E)[:, :, NT - 1]))
                link(dve.memset(ones8, 1.0))
                link(dve.tensor_copy(cstart[:, 1:E], cend[:, 0:E - 1]))
                link(dve.tensor_tensor(total, cend, cstart, ALU.subtract))
                et = work_a.rearrange("p (e t) -> p e t", e=E)
                link(dve.tensor_tensor(et, total.unsqueeze(2).broadcast_to([P, E, NT]),
                                       steps128[:].unsqueeze(1).broadcast_to([P, E, NT]), ALU.is_gt))
                link(dve.tensor_reduce(tiles, et, AX, ALU.add))
                link(dve.tensor_tensor_scan(tend, ones8, tiles, 0.0, ALU.mult, ALU.add))
                link(dve.tensor_tensor(tbase, tend, tiles, ALU.subtract))
                link(dve.scalar_tensor_tensor(out=off, in0=tbase, scalar=float(P), in1=cstart, op0=ALU.mult, op1=ALU.subtract))
                link(dve.tensor_tensor(work_b, work_b, of_tile, ALU.subtract))
                link(dve.tensor_tensor(work_b, work_b, in_tile, ALU.add))
                bt = work_b.rearrange("p (e t) -> p e t", e=E)
                link(dve.tensor_tensor(bt, bt, off.unsqueeze(2).broadcast_to([P, E, NT]), ALU.add))
                link(dve.tensor_tensor(wa, one_hot, te(work_b), ALU.mult))
                link(dve.tensor_reduce(slot_f[:], wa, AX, ALU.add))
                link(dve.tensor_copy(slot_i[:], slot_f[:]))
                link(dve.tensor_tensor(te_cmp, tile_no[:], tend[0:1].unsqueeze(1).broadcast_to([1, 40, E]), ALU.is_ge))
                link(dve.tensor_reduce(te_sum, te_cmp, AX, ALU.add))
                dve.tensor_scalar(tile_expert[:], te_sum, float(E - 1), None, ALU.min).then_inc(R["routed", L], 1)

                I, CW = FFN[L]["I"], FFN[L]["CW"]
                NCH = I // CW
                fch = Chain(dve, F["chain", L], 1, wait_carried)

                def f_stats(i, r, m):
                    fch.begin(i)
                    wait(dve, F["x_done", L], i)
                    dve.wait_ge(F["xs_loaded%d" % r, L], 16 * m + 16)
                    dve.sem_inc(wait_carried, 1)
                    fch.link(dve.bn_stats(f_st, xs[r][:]))
                    dve.bn_aggr(f_mv, f_st).then_inc(F["stats_done", L], 1)

                def f_apply(i, r):
                    dve.wait_ge(F["rstd_done", L], i + 1)
                    wait(dve, F["xT_ps", L], i)
                    dve.tensor_scalar(f_xn, xs[r][:], f_mv[:, 0:1], f_rstd, ALU.subtract, ALU.mult).then_inc(F["x_done", L], 1)

                def xT_evac(i):
                    dve.wait_ge(F["xT_ps", L], i + 1)
                    wait(dve, F["h_ps", L], NCH * i)
                    dve.tensor_copy(f_xT.rearrange("p a b -> p (a b)"), ps[:, 5, 0:D]).then_inc(F["xT_sb", L], 1)

                def hT_evac(i, n):
                    q = CW // P
                    dve.wait_ge(F["hT_ps", L], NCH * i + n + 1)
                    wait(dve, F["y_ps", L], i)
                    dve.tensor_copy(f_hT[:, n * q:(n + 1) * q, :].rearrange("p a b -> p (a b)"), ps[:, 2 + n, 0:CW]
                                    ).then_inc(F["hT_sb", L], 1)

                f_stats(0, 0, 0)
                f_apply(0, 0)
                xT_evac(0)
                f_stats(1, 1, 0)
                f_apply(1, 1)

                def tile(i, r, m):
                    left = SLOT_TILES - i if isinstance(i, int) else SLOT_TILES
                    if left > 1:
                        xT_evac(i + 1)
                    if left > 2:
                        f_stats(i + 2, (r + 2) % RING, m + (r + 2) // RING)
                    for n in range(NCH):
                        hT_evac(i, n)
                    if left > 2:
                        f_apply(i + 2, (r + 2) % RING)

                loop(dve, SLOT_TILES, tile, unroll=RING)

            with dve.Fori(0, NT // RG) as m:
                for r in range(RG):
                    dve.wait_ge(last_gathered[r], 16 * m + 16)
                    t = row(RG * m + r)
                    dve.scalar_tensor_tensor(out=t, in0=last_y[r], scalar=gates[:, bass.ds(RG * m + r, 1)], in1=t,
                                             op0=ALU.mult, op1=ALU.add).then_inc(last_added, 1)


_INS = ['x', 'ctx_1024', 'mask_BxSxS2_ff0', 'g_xattn', 'g_ffn', 'L0_xattn_w_q', 'L0_xattn_b_q', 'L0_xattn_w_kv',
        'L0_xattn_b_kv', 'L0_xattn_w_out', 'L0_xattn_b_out', 'L0_ffn_w1', 'L0_ffn_b1', 'L0_ffn_w2', 'L0_ffn_b2',
        'L0_ffn_wr', 'L0_ffn_br', 'L1_xattn_wq_kernel', 'L1_xattn_wq_bias', 'L1_xattn_wk_kernel', 'L1_xattn_wk_bias',
        'L1_xattn_wv_kernel', 'L1_xattn_wv_bias', 'L1_ffn_Wg', 'L1_ffn_bg', 'L1_ffn_W1', 'L1_ffn_b1', 'L1_ffn_W2',
        'L1_ffn_b2']


def kernel(**inputs):
    import numpy as _np
    import concourse.bacc as _bacc
    from concourse import mybir as _mybir
    from concourse.bass_utils import run_bass_kernel_spmd as _run

    nc = _bacc.Bacc("TRN2", target_bir_lowering=False, num_devices=1)
    arrays, args = {}, []
    for name in _INS:
        a = _np.ascontiguousarray(inputs[name])
        arrays[f"in_{name}_dram"] = a
        args.append(nc.dram_tensor(f"in_{name}_dram", a.shape, _mybir.dt.from_np(a.dtype), kind="ExternalInput").ap())
    args.append(nc.dram_tensor("out_0_dram", (NB, S, D), _mybir.dt.float32, kind="ExternalOutput").ap())
    flamingo_kernel(nc, *args)
    r = _run(nc, [arrays], core_ids=[0])
    return r.results[0]["out_0_dram"]
```

```python
from contextlib import ExitStack

import concourse.bass as bass
from concourse import mybir

ALU = mybir.AluOpType
ACT = mybir.ActivationFunctionType
F32 = mybir.dt.float32
BF16 = mybir.dt.bfloat16
I32 = mybir.dt.int32
AX = mybir.AxisListType.X

P = 128
NB, S, D, Z = 16, 256, 256, 77
NC = D // P
TPB = S // P
NT = NB * TPB
E = 8
SLOT_TILES = (NB * S + E * (P - 1)) // P
REGION = NB * S + P
MIN_TILES = NB * S // P
NROWS = E * REGION + (SLOT_TILES - MIN_TILES) * P
EPS = 1e-5
RING = 5
ROW = D + 2
HG = 4
GZ = HG * Z
LG0 = GZ
RK0 = LG0 + TPB * E
CT0 = RK0 + TPB * E

ATT = {
    0: dict(H=16, hpc=8, units=4, mask_val=1e12),
    1: dict(H=8, hpc=4, units=2, mask_val=1e9),
}
FFN = {0: dict(I=1024, CW=512), 1: dict(I=256, CW=256)}


def wait(eng, sem, value):
    if isinstance(value, int) and value <= 0:
        return
    eng.wait_ge(sem, value)


class Chain:

    def __init__(self, eng, sem, apart=None):
        self.eng, self.sem, self.apart = eng, sem, apart

    def begin(self, before):
        self.made = before

    def link(self, ins):
        self.made = self.made + 1
        ins.then_inc(self.sem, 1)
        self.eng.wait_ge(self.sem, self.made)
        if self.apart is not None:
            self.eng.sem_inc(self.apart, 1)


def loop(eng, n, step, unroll=1, head=1, tail=1):
    for i in range(head * unroll):
        step(i, i % unroll, i // unroll)
    end = n // unroll - tail
    with eng.Fori(head, end) as m:
        for r in range(unroll):
            step(m * unroll + r, r, m)
    for i in range(end * unroll, n):
        step(i, i % unroll, i // unroll)


def before(i, n):
    return not isinstance(i, int) or i < n


def since(i, n):
    return not isinstance(i, int) or i >= n


def upto(i, n):
    return min(i, n) if isinstance(i, int) else i


def flamingo_kernel(nc, x, ctx_in, mask, g_xattn, g_ffn,
                    w_q0, b_q0, w_kv0, b_kv0, w_o0, b_o0, w1_0, b1_0, w2_0, b2_0, wr0, br0,
                    w_q1, b_q1, w_k1, b_k1, w_v1, b_v1, wr1, br1, w1_1, b1_1, w2_1, b2_1, out):
    with ExitStack() as ctx:
        def sb(name, shape, dt=F32):
            return ctx.enter_context(nc.sbuf_tensor(name, shape, dt))

        def sem(name):
            return ctx.enter_context(nc.semaphore(name))

        slots_dram = nc.dram_tensor("slot_rows", (NROWS, ROW), F32, kind="Internal").ap()
        xmid_dram = nc.dram_tensor("x_between_layers", (NB * S, D), F32, kind="Internal").ap()

        xres = sb("xres", [P, NT, ROW])
        w1sb = sb("w1sb", [P, E * NC, 1024])
        w2sb = sb("w2sb", [P, E * 8, D])
        wq, wk, wv, wo = (sb(n, [P, NC, D]) for n in ("wq", "wk", "wv", "wo"))
        bq, bk = sb("bq", [P, NC]), sb("bk", [P, NC])
        bv = sb("bv", [Z, D])
        tg = sb("tg", [P, 4])
        ident = sb("ident", [P, P])
        headmask = {0: sb("headmask0", [P, 8]), 1: sb("headmask1", [P, 4])}
        maskneg = sb("maskneg", [P, TPB, Z])
        wr = sb("wr", [P, NC, E])
        brb = sb("brb", [P, E])
        gate_new = sb("gate_new", [P, TPB])
        slot_i = sb("slot_i", [P, NT], I32)
        tile_expert = sb("tile_expert", [1, 40], I32)
        tile_row = sb("tile_row", [1, 40], I32)
        pad_row = sb("pad_row", [1, E], I32)
        expert_rows = sb("expert_rows", [96, E, P], BF16)
        biasw = sb("biasw", [96, 1024 + D], BF16)
        halfneg = sb("halfneg", [P, TPB])
        eps = sb("eps", [P, TPB])
        gated_bo = sb("gated_bo", [P, D])
        pad_rows = sb("pad_rows", [P, ROW])
        token_f, token_i = sb("token_f", [P, 1]), sb("token_i", [P, RING], I32)

        SCRATCH = 7144
        scratch = sb("scratch", [P, SCRATCH])

        def carve(*shapes):
            at, got = 0, []
            for shape in shapes:
                n = 1
                for s in shape[1:]:
                    n *= s
                ap = scratch[0:shape[0], at:at + n]
                if len(shape) == 3:
                    ap = ap.rearrange("p (a b) -> p a b", a=shape[1])
                got.append(ap)
                at += n
            assert at <= SCRATCH, at
            return got

        (xhat, xT, ctxs, cT, qT, kbd, vaug, vnext, p0, p1, pt0, pt1, attn, attnT, xst, mv, veps, rstd, mx, rinv,
         r_x, r_st, r_mv, r_veps, r_rstd, lg, is_top, slot_of, tmax, tmax2, slot_f
         ) = carve([P, TPB, D], [P, NC, S], [Z, D], [P, NC, Z], [P, NC, S], [P, NC, 8 * Z], [Z, 16 * 17], [Z, 16 * 17],
                   [P, 2, GZ], [P, 2, GZ], [Z, HG, P], [Z, HG, P], [P, D], [P, NC, P],
                   [P, TPB, 6], [P, TPB, 2], [P, TPB], [P, TPB], [P, 2 * HG], [P, 16],
                   [P, TPB, D], [P, TPB, 6], [P, TPB, 2], [P, TPB], [P, TPB], [P, TPB, E], [P, TPB, E], [P, TPB, E],
                   [P, TPB], [P, TPB], [P, TPB])
        p_sb, pt_sb = [p0, p1], [pt0, pt1]
        rawmask = attnT.rearrange("p a b -> p (a b)")[:, 0:TPB * Z].rearrange("p (a b) -> p a b", a=TPB)
        r_flat = r_x.rearrange("p a b -> p (a b)")
        steps_below = r_flat[:, 0:NT * E].rearrange("p (a b) -> p a b", a=E)
        te_cmp = r_flat[0:1, 0:40 * E].rearrange("p (a b) -> p a b", a=40)
        te_sum = r_flat[0:1, 40 * E:40 * E + 40]
        total, tiles, tend, ones8, delta = (r_flat[:, 40 * (E + 1) + q * E:40 * (E + 1) + (q + 1) * E] for q in range(5))
        one_hot = sb("one_hot", [P, TPB, E], BF16)
        row_base = sb("row_base", [P, E])
        region0 = sb("region0", [P, E])
        upper = sb("upper", [P, P], BF16)
        ones_b = sb("ones_b", [P, P], BF16)
        exp_rev = sb("exp_rev", [P, E])
        steps128 = sb("steps128", [P, NT])
        tile_no = sb("tile_no", [1, 40])
        (f_xn, f_xT, f_h, f_hT, f_st, f_mv, f_veps, f_rstd, *f_rows
         ) = carve([P, D], [P, NC, P], [P, 1024], [P, 8, P], [P, 6], [P, 2], [P, 1], [P, 1], *[[P, ROW]] * RING, *[[P, D]] * RING)
        xs, f_y = f_rows[0:RING], f_rows[RING:]
        biasf = {0: w1sb[0:96, 14:16, :].rearrange("p a b -> p (a b)"), 1: w1sb[0:96, 0, 256:768]}

        ps = ctx.enter_context(nc.psum_tensor("ps", [P, 8, 512], F32))

        const_loaded = sem("const_loaded")
        late_loaded = sem("late_loaded")
        const_made, const_chain, tanh_done, tgb_done = sem("const_made"), sem("const_chain"), sem("tanh_done"), sem("tgb_done")
        zeros_made, zero_stored, weights_loaded = sem("zeros_made"), sem("zero_stored"), {0: sem("weights_loaded0"), 1: sem("weights_loaded1")}
        a_rstd_chain, r_rstd_chain, f_rstd_chain, norm_link, rows_link, experts_link = (
            sem(n) for n in ("a_rstd_chain", "r_rstd_chain", "f_rstd_chain", "norm_link", "rows_link", "experts_link"))
        A = {}
        for L in (0, 1):
            for n in ("x_loaded", "ctx_loaded", "mask_loaded", "stats_done", "rstd_done", "xhat_done",
                      "prep_chain", "sm_chain", "xT_ps", "xT_sb", "cT_ps", "cT_sb", "q_ps", "q_sb", "kv_ps", "kbd_done",
                      "v_evac", "v_done", "mask_done", "s_ps", "sub_done", "exp_done", "pt_ps", "pt_sb", "av_ps", "attn_done", "at_ps", "at_sb",
                      "wo_ps", "res_done", "bo_done"):
                if L == 0 and n.startswith("mask") or L == 1 and n in ("at_ps", "at_sb", "wo_ps", "bo_done"):
                    continue
                A[n, L] = sem(f"a{L}_{n}")
        R = {(n, L): sem(f"r{L}_{n}") for L in (0, 1) for n in (
            "stats_done", "rstd_done", "x_done", "xT_ps", "xT_sb", "lg_ps", "lg_done", "onehot_done",
            "slot_done", "gap_done", "gate_exp", "route_chain", "pads_known", "routed", "scattered", "pads_stored")
             if L == 0 or n not in ("gap_done", "gate_exp")}
        F = {(n, L): sem(f"f{L}_{n}") for L in (0, 1) for n in (
            ["stats_done", "rstd_done", "x_done", "xT_ps", "xT_sb", "h_ps", "h_sb", "hT_ps", "hT_sb",
             "y_ps", "y_sb"])}
        xs_loaded = [sem(f"xs_loaded{r}") for r in range(RING)]
        y_scattered = [sem(f"y_scattered{r}") for r in range(RING)]
        bias_zeroed, bias_loaded, bias_split, bias_link, vaug_ones = (
            sem(n) for n in ("bias_zeroed", "bias_loaded", "bias_split", "bias_link", "vaug_ones"))
        bq_done = sem("bq_done")
        wait_carried, pool_wait_carried = sem("wait_carried"), sem("pool_wait_carried")
        tokens_done = sem("tokens_done")

        def uses(r):
            return (SLOT_TILES - r + RING - 1) // RING

        def rows_back(eng, L):
            for r in range(RING):
                eng.wait_ge(y_scattered[r], 16 * uses(r) * (L + 1))


        consts_there, late_there = {0: 16 * 6, 1: 16 * 12}, {0: 16 * 6, 1: 16 * 8}

        def store_pads(eng, L, experts):
            for e in experts:
                r = eng.value_load(pad_row[0:1, e:e + 1], min_val=0, max_val=E * REGION - P)
                eng.dma_start(slots_dram[bass.ds(r, P), :], pad_rows[:]).then_inc(R["pads_stored", L], 16)

        block = ctx.enter_context(nc.Block())

        @block.sync
        def _(sp):
            def rows(w):
                return w.rearrange("(c p) n -> p c n", p=P)

            def cols(b):
                return b.rearrange("(c p) -> p c", p=P)

            def load_batch(L, b):
                wait(sp, A["x_loaded", L], 16 * b)
                src = x if L == 0 else xmid_dram.rearrange("(b s) d -> b s d", b=NB)
                sp.dma_start(xres[:, bass.ds(TPB * b, TPB), 0:D],
                             src[bass.ds(b, 1), :, :].rearrange("a (j p) d -> p (a j) d", p=P)).then_inc(A["x_loaded", L], 16)
                wait(sp, A["cT_ps", L], b)
                sp.dma_start(ctxs, ctx_in[bass.ds(b, 1), :, :].rearrange("a z d -> (a z) d")).then_inc(A["ctx_loaded", L], 16)
                if L == 1:
                    wait(sp, A["mask_done", L], b)
                    sp.dma_start(rawmask, mask[bass.ds(b, 1), :, :].rearrange("a (j p) z -> p (a j) z", p=P)
                                 ).then_inc(A["mask_loaded", L], 16)

            def load_consts(L):
                q, late = const_loaded, late_loaded
                wk_src, wv_src = (w_kv0[:, 0:D], w_kv0[:, D:2 * D]) if L == 0 else (w_k1, w_v1)
                sp.dma_start(wq[:], rows(w_q0 if L == 0 else w_q1)).then_inc(q, 16)
                sp.dma_start(bq[:], cols(b_q0 if L == 0 else b_q1), allow_slow_non_contiguous=True).then_inc(q, 16)
                sp.dma_start(wk[:], rows(wk_src)).then_inc(q, 16)
                sp.dma_start(wv[:], rows(wv_src)).then_inc(q, 16)
                sp.dma_start(bk[:], cols(b_kv0[0:D] if L == 0 else b_k1), allow_slow_non_contiguous=True).then_inc(q, 16)
                sp.dma_start(bv[:], (b_kv0[D:2 * D] if L == 0 else b_v1).partition_broadcast(Z)).then_inc(q, 16)
                if L == 0:
                    sp.dma_start(tg[:, 0:2], g_xattn.partition_broadcast(P)).then_inc(late, 16)
                    sp.dma_start(tg[:, 2:4], g_ffn.partition_broadcast(P)).then_inc(late, 16)
                    sp.dma_start(gated_bo[:], b_o0.partition_broadcast(P)).then_inc(late, 16)
                    sp.dma_start(wo[:], rows(w_o0)).then_inc(late, 16)
                sp.dma_start(wr[:], rows(wr0 if L == 0 else wr1)).then_inc(late, 16)
                sp.dma_start(brb[:], (br0 if L == 0 else br1).partition_broadcast(P)).then_inc(late, 16)

            def load_biases(L):
                b1, b2 = (b1_0, b2_0) if L == 0 else (b1_1, b2_1)
                I = FFN[L]["I"]
                sp.wait_ge(bias_zeroed, L + 1)
                for q in range(3):
                    sp.dma_start(biasf[L][32 * q:32 * q + E, 0:I], b1).then_inc(bias_loaded, 16)
                    sp.dma_start(biasf[L][32 * q:32 * q + E, I:I + D], b2).then_inc(bias_loaded, 16)

            def load_weights(L, b):
                wait(sp, weights_loaded[L], 32 * b)
                if L == 0:
                    sp.dma_start(w1sb[:, bass.ds(b, 1), :],
                                 w1_0.rearrange("e (c p) n -> (e c) p n", p=P)[bass.ds(b, 1), :, :].rearrange("a p n -> p a n")
                                 ).then_inc(weights_loaded[L], 16)
                    sp.dma_start(w2sb[:, bass.ds(4 * b, 4), :],
                                 w2_0.rearrange("e (c p) n -> (e c) p n", p=P)[bass.ds(4 * b, 4), :, :].rearrange("a p n -> p a n")
                                 ).then_inc(weights_loaded[L], 16)
                else:
                    for dst, src in ((w1sb[:, :, 0:D], w1_1), (w2sb, w2_1)):
                        sp.dma_start(dst[:, bass.ds(b, 1), :],
                                     src.rearrange("e (c p) n -> (e c) p n", p=P)[bass.ds(b, 1), :, :].rearrange("a p n -> p a n")
                                     ).then_inc(weights_loaded[L], 16)

            def experts_io(L):
                sp.wait_ge(R["pads_known", L], 1)
                sp.wait_ge(zeros_made, 1)
                store_pads(sp, L, range(0, E, 2))
                sp.wait_ge(R["routed", L], 1)
                sp.wait_ge(R["scattered", L], 16 * NT)
                sp.wait_ge(R["pads_stored", L], 16 * E)
                if L == 0:
                    sp.wait_ge(zero_stored, 16)

                def row_of(i):
                    return bass.ds(sp.value_load(tile_row[0:1, bass.ds(i, 1)], min_val=0, max_val=NROWS - P), P)

                for i in range(RING - 1):
                    sp.dma_start(xs[i][:], slots_dram[row_of(i), :]).then_inc(xs_loaded[i], 16)
                if L == 0:
                    load_consts(1)

                def step(i, r, m):
                    if not isinstance(i, int) or i + RING - 1 < SLOT_TILES:
                        wait(sp, F["y_sb", L], i)
                        r4 = (r + RING - 1) % RING
                        sp.dma_start(xs[r4][:], slots_dram[row_of(i + RING - 1), :]).then_inc(xs_loaded[r4], 16)

                loop(sp, SLOT_TILES, step, unroll=RING, tail=0)

            for L in (0, 1):
                if L == 0:
                    load_batch(0, 0)
                    load_consts(0)
                else:
                    rows_back(sp, 0)
                    load_batch(1, 0)
                load_biases(L)
                load_weights(L, 0)
                with sp.Fori(1, 14) as b:
                    load_batch(L, b)
                    load_weights(L, b)
                sp.wait_ge(bias_split, L + 1)
                for b in (14, 15):
                    load_batch(L, b)
                    load_weights(L, b)
                experts_io(L)

            rows_back(sp, 1)

        @block.gpsimd
        def _(pool):
            c = [0]

            def link(ins):
                c[0] += 1
                ins.then_inc(const_chain, 1)
                pool.wait_ge(const_chain, c[0])

            pool.memset(pad_rows[:, 0:D + 1], 0.0)
            pool.memset(pad_rows[:, D + 1:ROW], float(NB * S)).then_inc(zeros_made, 1)
            pool.iota(token_f[:], pattern=[[0, 1]], base=0, channel_multiplier=1, allow_small_or_imprecise_dtypes=True
                      ).then_inc(tokens_done, 1)
            pool.wait_ge(tokens_done, 1)
            pool.iota(xres[:, :, D + 1], pattern=[[P, NT]], base=0, channel_multiplier=1, allow_small_or_imprecise_dtypes=True)
            for t in (ident, expert_rows, maskneg):
                pool.memset(t[:], 0.0)
            for t in (headmask[0], headmask[1], upper, ones_b):
                pool.memset(t[:], 1.0)
            pool.memset(eps[:], EPS)
            link(pool.memset(halfneg[:], -0.5))
            pool.affine_select(ident[:], ident[:], pattern=[[-1, P]], compare_op=ALU.not_equal, fill=1.0, base=0,
                               channel_multiplier=1)
            for L in (0, 1):
                n, d = ATT[L]["hpc"], P // ATT[L]["hpc"]
                link(pool.affine_select(headmask[L][:], headmask[L][:], pattern=[[-d, n]], compare_op=ALU.is_ge,
                                        fill=0.0, base=0, channel_multiplier=1))
                link(pool.affine_select(headmask[L][:], headmask[L][:], pattern=[[d, n]], compare_op=ALU.is_ge,
                                        fill=0.0, base=d - 1, channel_multiplier=-1))
            pool.affine_select(maskneg[:, 0, :], maskneg[:, 0, :], pattern=[[-1, Z]], compare_op=ALU.is_gt,
                               fill=-ATT[0]["mask_val"], base=0, channel_multiplier=1).then_inc(const_made, 1)
            for q in range(3):
                link(pool.affine_select(expert_rows[:], expert_rows[:], pattern=[[-1, E], [0, P]],
                                        compare_op=ALU.not_equal, fill=1.0, base=-32 * q, channel_multiplier=1))
            pool.affine_select(upper[:], upper[:], pattern=[[1, P]], compare_op=ALU.is_gt, fill=0.0, base=0,
                               channel_multiplier=-1)
            pool.iota(exp_rev[:], pattern=[[-1, E]], base=E, channel_multiplier=0, allow_small_or_imprecise_dtypes=True)
            pool.iota(region0[:], pattern=[[REGION, E]], base=0, channel_multiplier=0, allow_small_or_imprecise_dtypes=True)
            pool.iota(row_base[:], pattern=[[REGION, E]], base=0, channel_multiplier=0, allow_small_or_imprecise_dtypes=True)
            pool.iota(steps128[:], pattern=[[P, NT]], base=0, channel_multiplier=0, allow_small_or_imprecise_dtypes=True)
            pool.iota(tile_no[:], pattern=[[1, 40]], base=0, channel_multiplier=0,
                      allow_small_or_imprecise_dtypes=True).then_inc(const_made, 1)

            def make_rstd(stats_done, chain, past, done, step, var, plus_eps, rs, n):
                pool.wait_ge(stats_done, step + 1)
                pool.tensor_tensor(plus_eps, var, eps[:, 0:n], ALU.add).then_inc(chain, 1)
                pool.wait_ge(chain, past + step + 1)
                pool.tensor_tensor(rs, plus_eps, halfneg[:, 0:n], ALU.pow).then_inc(done, 1)

            for L in (0, 1):
                U = ATT[L]["units"]

                def rstd_batch(b):
                    make_rstd(A["stats_done", L], a_rstd_chain, NB * L, A["rstd_done", L], b, mv[:, :, 1], veps, rstd, TPB)

                def rstd_rows(k):
                    make_rstd(R["stats_done", L], r_rstd_chain, NB * L, R["rstd_done", L], k, r_mv[:, :, 1], r_veps, r_rstd, TPB)

                def scatter(k):
                    pool.wait_ge(R["slot_done", L], k + 1)
                    for t in range(TPB * k, TPB * k + TPB):
                        pool.indirect_dma_start(slots_dram, bass.IndirectOffsetOnAxis(ap=slot_i[:, t:t + 1], axis=0),
                                                xres[:, t, :], None).then_inc(R["scattered", L], 16)

                def add_bias(b, j):
                    pool.wait_ge(A["res_done", 0], TPB * b + j + 1)
                    t = xres[:, bass.ds(TPB * b + j, 1), 0:D].rearrange("p a d -> p (a d)")
                    pool.tensor_tensor(t, t, gated_bo[:], ALU.add).then_inc(A["bo_done", 0], 1)

                def use_v(b):
                    wait(pool, A["av_ps", L], U * b)
                    pool.wait_ge(A["v_evac", L], b + 1)
                    pool.sem_inc(pool_wait_carried, 1)
                    pool.tensor_copy(vaug, vnext).then_inc(A["v_done", L], 1)

                if L == 0:
                    rstd_batch(0)
                    use_v(0)
                    pool.wait_ge(tanh_done, 1)
                    pool.tensor_scalar(gated_bo[:], gated_bo[:], tg[:, 0:1], None, ALU.mult).then_inc(tgb_done, 1)
                    pool.wait_ge(tgb_done, 1)
                    rstd_batch(1)

                    for b in range(NB):
                        if b > 0:
                            add_bias(b - 1, 1)
                            rstd_rows(b - 1)
                        if b > 2:
                            scatter(b - 3)
                        if b < NB - 2:
                            rstd_batch(b + 2)
                        add_bias(b, 0)
                        if b < NB - 1:
                            use_v(b + 1)
                    add_bias(NB - 1, 1)
                else:
                    rstd_batch(0)
                    rstd_batch(1)
                    use_v(0)
                    rstd_batch(2)
                    for b in range(NB):
                        if b > 0:
                            rstd_rows(b - 1)
                        if b + 3 < NB:
                            rstd_batch(b + 3)
                        if b + 1 < NB:
                            use_v(b + 1)
                        if b > 2:
                            scatter(b - 3)

                rstd_rows(NB - 1)
                for k in range(NB - 3, NB):
                    scatter(k)

                def rstd_tile(i):
                    make_rstd(F["stats_done", L], f_rstd_chain, SLOT_TILES * L, F["rstd_done", L], i, f_mv[:, 1:2], f_veps, f_rstd, 1)

                def scatter_tile(i, r, m):
                    if not isinstance(i, int) or i + 3 < SLOT_TILES:
                        rstd_tile(i + 3)
                    pool.wait_ge(F["y_sb", L], i + 1)
                    pool.sem_inc(pool_wait_carried, 1)
                    dst = xmid_dram if L == 0 else out.rearrange("b s d -> (b s) d")
                    pool.indirect_dma_start(dst, bass.IndirectOffsetOnAxis(ap=token_i[:, r:r + 1], axis=0), f_y[r], None,
                                            bounds_check=NB * S - 1, oob_is_err=False).then_inc(y_scattered[r], 16)

                for i in range(3):
                    rstd_tile(i)
                loop(pool, SLOT_TILES, scatter_tile, unroll=RING, tail=0)


        @block.scalar
        def _(act):

            for L in (0, 1):
                U = ATT[L]["units"]
                act.wait_ge(const_loaded, consts_there[L])
                if L == 1:
                    act.activation(bq[:], bq[:], ACT.Copy, scale=(D // ATT[1]["H"]) ** -0.5).then_inc(bq_done, 1)
                    act.wait_ge(bq_done, 1)

                def xT_evac(b):
                    act.wait_ge(A["xT_ps", L], b + 1)
                    wait(act, A["q_ps", L], b)
                    wait(act, R["lg_ps", L], b - 2 if L == 0 else b - 3)
                    act.activation(xT.rearrange("p a b -> p (a b)"), ps[:, 7, :], ACT.Copy).then_inc(A["xT_sb", L], 1)

                def cT_evac(b):
                    act.wait_ge(A["cT_ps", L], b + 1)
                    wait(act, A["kv_ps", L], b)
                    act.activation(cT.rearrange("p a b -> p (a b)"), ps[:, 7, 0:NC * Z], ACT.Copy).then_inc(A["cT_sb", L], 1)

                def q_evac(b):
                    act.wait_ge(A["q_ps", L], b + 1)
                    wait(act, A["s_ps", L], U * b)
                    for f in range(NC):
                        ins = act.activation(qT[:, f, :], ps[:, 7, f * S:(f + 1) * S], ACT.Identity, bias=bq[:, f:f + 1],
                                             scale=1.0 if L == 0 else (D // ATT[1]["H"]) ** -0.5)
                    ins.then_inc(A["q_sb", L], 1)

                def exp_unit(b, u):
                    n = U * b + u
                    act.wait_ge(A["sub_done", L], n + 1)
                    act.activation(p_sb[u % 2], p_sb[u % 2], ACT.Exp).then_inc(A["exp_done", L], 1)

                def pt_evac(b, u):
                    n = U * b + u
                    for g in range(2):
                        act.wait_ge(A["pt_ps", L], 2 * n + g + 1)
                        if g == 0:
                            wait(act, A["av_ps", L], n)
                        act.activation(pt_sb[g].rearrange("p a b -> p (a b)"), ps[0:Z, 4 + g, :], ACT.Copy
                                       ).then_inc(A["pt_sb", L], 1)

                def exp_gap(k):
                    act.wait_ge(R["gap_done", 0], k + 1)
                    act.activation(gate_new[:], gate_new[:], ACT.Exp).then_inc(R["gate_exp", 0], 1)

                def attnT_evac(b, j):
                    act.wait_ge(A["at_ps", L], TPB * b + j + 1)
                    wait(act, A["wo_ps", L], TPB * b + j)
                    act.activation(attnT.rearrange("p a b -> p (a b)"), ps[:, 7, 0:D], ACT.Copy).then_inc(A["at_sb", L], 1)

                def rT_evac(k):
                    act.wait_ge(R["xT_ps", L], k + 1)
                    wait(act, A["q_ps", L], upto(k + (3 if L == 0 else 4), NB))
                    wait(act, R["lg_ps", L], k)
                    act.activation(xT.rearrange("p a b -> p (a b)"), ps[:, 7, :], ACT.Copy).then_inc(R["xT_sb", L], 1)

                xT_evac(0)
                cT_evac(0)
                q_evac(0)
                if L == 0:
                    act.wait_ge(late_loaded, late_there[0])
                    act.activation(tg[:], tg[:], ACT.Tanh).then_inc(tanh_done, 1)
                    act.wait_ge(zeros_made, 1)
                    act.dma_start(slots_dram[E * REGION:NROWS, :].rearrange("(n p) d -> p n d", p=P),
                                  pad_rows[:].unsqueeze(1).broadcast_to([P, SLOT_TILES - MIN_TILES, ROW])).then_inc(zero_stored, 16)
                exp_unit(0, 0)
                if L == 1:
                    exp_unit(0, 1)
                    xT_evac(1)
                    cT_evac(1)
                    q_evac(1)

                def batch0(b, _r, _m):
                    nxt = before(b, NB - 1)
                    if since(b, 2):
                        rT_evac(b - 2)
                    pt_evac(b, 0)
                    if not isinstance(b, int) or b > 0:
                        attnT_evac(b - 1, 1)
                    exp_unit(b, 1)
                    exp_unit(b, 2)
                    pt_evac(b, 1)
                    if nxt:
                        xT_evac(b + 1)
                        cT_evac(b + 1)
                    exp_unit(b, 3)
                    if nxt:
                        q_evac(b + 1)
                    pt_evac(b, 2)
                    if since(b, 2):
                        exp_gap(b - 2)
                    attnT_evac(b, 0)
                    pt_evac(b, 3)
                    if nxt:
                        exp_unit(b + 1, 0)

                def batch1(b, _r, _m):
                    pt_evac(b, 0)
                    if since(b, 2):
                        rT_evac(b - 2)
                    if before(b, NB - 2):
                        xT_evac(b + 2)
                    if before(b, NB - 1):
                        exp_unit(b + 1, 0)
                    if before(b, NB - 2):
                        cT_evac(b + 2)
                    pt_evac(b, 1)
                    if before(b, NB - 2):
                        q_evac(b + 2)
                    if before(b, NB - 1):
                        exp_unit(b + 1, 1)

                if L == 0:
                    loop(act, NB, batch0, head=3)
                    rT_evac(NB - 2)
                    attnT_evac(NB - 1, 1)
                    rT_evac(NB - 1)
                    exp_gap(NB - 2)
                    exp_gap(NB - 1)
                else:
                    loop(act, NB, batch1, head=3, tail=2)
                    rT_evac(NB - 2)
                    rT_evac(NB - 1)

                act.wait_ge(R["pads_known", L], 1)
                act.wait_ge(zeros_made, 1)
                store_pads(act, L, range(1, E, 2))

                I, CW = FFN[L]["I"], FFN[L]["CW"]
                NCH = I // CW

                def gelu(i, n):
                    act.wait_ge(F["h_ps", L], NCH * i + n + 1)
                    wait(act, F["hT_ps", L], NCH * (i - 1) + n + 1)
                    act.activation(f_h[:, n * CW:(n + 1) * CW], ps[:, n, 0:CW], ACT.Gelu).then_inc(F["h_sb", L], 1)

                for n in range(NCH):
                    gelu(0, n)

                def tile(i, r, m):
                    if not isinstance(i, int) or i + 1 < SLOT_TILES:
                        for n in range(NCH):
                            gelu(i + 1, n)

                loop(act, SLOT_TILES, tile)

        @block.tensor
        def _(pe):
            pe.wait_ge(const_made, 2)
            for L in (0, 1):
                U, H, hpc = (ATT[L][k] for k in ("units", "H", "hpc"))
                d = D // H

                def turn_x(b):
                    pe.wait_ge(A["xhat_done", L], b + 1)
                    wait(pe, A["v_evac", L], b)
                    if L == 0:
                        wait(pe, A["res_done", 0], TPB * (b - 1))
                    else:
                        wait(pe, R["xT_sb", L], b - 3)
                    for c in range(NC):
                        for j in range(TPB):
                            ins = pe.transpose(ps[:, 7, c * S + j * P:c * S + (j + 1) * P], xhat[:, j, c * P:(c + 1) * P], ident[:])
                    ins.then_inc(A["xT_ps", L], 1)

                def turn_ctx(b):
                    pe.wait_ge(A["ctx_loaded", L], 16 * b + 16)
                    pe.wait_ge(A["xT_sb", L], b + 1)
                    for c in range(NC):
                        ins = pe.transpose(ps[:, 7, c * Z:(c + 1) * Z], ctxs[:, c * P:(c + 1) * P], ident[0:Z, 0:Z])
                    ins.then_inc(A["cT_ps", L], 1)

                def project_q(b):
                    pe.wait_ge(A["cT_sb", L], b + 1)
                    if isinstance(b, int) and b == 0:
                        pe.wait_ge(const_loaded, consts_there[L])
                    for f in range(NC):
                        for k in range(NC):
                            ins = pe.matmul(ps[:, 7, f * S:(f + 1) * S], wq[:, k, f * P:(f + 1) * P], xT[:, k, :],
                                            start=(k == 0), stop=(k == NC - 1))
                    ins.then_inc(A["q_ps", L], 1)

                def project_kv(b):
                    pe.wait_ge(A["q_sb", L], b + 1)
                    for f in range(NC):
                        for k in range(NC):
                            pe.matmul(ps[:, 7, f * Z:(f + 1) * Z], wk[:, k, f * P:(f + 1) * P], cT[:, k, :],
                                      start=(k == 0), stop=(k == NC - 1))
                    for k in range(NC):
                        ins = pe.matmul(ps[0:Z, 7, D:2 * D], cT[:, k, :], wv[:, k, :], start=(k == 0), stop=(k == NC - 1))
                    ins.then_inc(A["kv_ps", L], 1)

                def scores(b, u):
                    n, buf = U * b + u, u % 2
                    if u == 0:
                        pe.wait_ge(A["kbd_done", L], b + 1)
                        pe.wait_ge(A["q_sb", L], b + 1)
                    wait(pe, A["sub_done", L], n - 1)
                    if L == 0 and u == 1:
                        wait(pe, R["lg_done", L], b - 2)
                    for g in range(2):
                        if L == 0:
                            lhs, rhs = qT[:, u % 2, (u // 2) * P:(u // 2 + 1) * P], kbd[:, u % 2, g * GZ:(g + 1) * GZ]
                        else:
                            lhs, rhs = qT[:, g, u * P:(u + 1) * P], kbd[:, g, 0:GZ]
                        ins = pe.matmul(ps[:, 2 * buf + g, 0:GZ], lhs, rhs, start=True, stop=True)
                    ins.then_inc(A["s_ps", L], 1)

                def turn_p(b, u):
                    n = U * b + u
                    pe.wait_ge(A["exp_done", L], n + 1)
                    for g in range(2):
                        wait(pe, A["pt_sb", L], 2 * n + g - 1)
                        for k in range(HG):
                            ins = pe.transpose(ps[0:Z, 4 + g, k * P:(k + 1) * P], p_sb[u % 2][:, g, k * Z:(k + 1) * Z], ident[:])
                        ins.then_inc(A["pt_ps", L], 1)

                def weigh_v(b, u):
                    n = U * b + u
                    j, first = (u // 2, u % 2 == 0) if L == 0 else (u, True)
                    if u == 0:
                        pe.wait_ge(A["v_done", L], b + 1)
                    if first:
                        wait(pe, A["attn_done", L], TPB * b + j)
                    for g in range(2):
                        pe.wait_ge(A["pt_sb", L], 2 * n + g + 1)
                        for k in range(HG):
                            h = (u % 2) * 8 + g * HG + k if L == 0 else g * HG + k
                            ins = pe.matmul(ps[:, 6, h * (d + 1):(h + 1) * (d + 1)], pt_sb[g][:, k, :],
                                            vaug[:, h * (d + 1):(h + 1) * (d + 1)], start=True, stop=True)
                    ins.then_inc(A["av_ps", L], 1)

                def turn_attn(b, j):
                    if j == 0 and before(b, NB - 1):
                        pe.wait_ge(A["v_evac", L], b + 2)
                    else:
                        wait(pe, A["res_done", L], TPB * b + j)
                    if j == 1:
                        wait(pe, R["xT_sb", L], upto(b, NB - 1))
                    pe.wait_ge(A["attn_done", L], TPB * b + j + 1)
                    for c in range(NC):
                        ins = pe.transpose(ps[:, 7, c * P:(c + 1) * P], attn[:, c * P:(c + 1) * P], ident[:])
                    ins.then_inc(A["at_ps", L], 1)

                def project_out(b, j):
                    pe.wait_ge(A["at_sb", L], TPB * b + j + 1)
                    for k in range(NC):
                        ins = pe.matmul(ps[:, 7, 0:D], attnT[:, k, :], wo[:, k, :], start=(k == 0), stop=(k == NC - 1))
                    ins.then_inc(A["wo_ps", L], 1)

                def turn_rows(k):
                    pe.wait_ge(R["x_done", L], k + 1)
                    if L == 0:
                        wait(pe, A["res_done", L], upto(TPB * (k + 1) + 1, NT))
                    else:
                        wait(pe, A["v_evac", L], upto(k + 4, NB))
                    wait(pe, R["xT_sb", L], k)
                    for c in range(NC):
                        for j in range(TPB):
                            ins = pe.transpose(ps[:, 7, c * S + j * P:c * S + (j + 1) * P], r_x[:, j, c * P:(c + 1) * P], ident[:])
                    ins.then_inc(R["xT_ps", L], 1)

                def route(k):
                    wait(pe, A["sub_done", L], upto(U * (k + 2) + 2, U * NB))
                    wait(pe, R["lg_done", L], k)
                    if before(k, NB):
                        pe.wait_ge(R["xT_sb", L], k + 1)
                        for j in range(TPB):
                            for c in range(NC):
                                ins = pe.matmul(ps[:, 2, LG0 + j * E:LG0 + (j + 1) * E], xT[:, c, j * P:(j + 1) * P], wr[:, c, :],
                                                start=(c == 0), stop=(c == NC - 1))
                    if since(k, 1):
                        pe.wait_ge(R["onehot_done", L], k)
                        flat = one_hot[:].rearrange("p a b -> p (a b)")
                        for j in range(TPB):
                            for q in range(j + 1):
                                pe.matmul(ps[:, 2, RK0 + j * E:RK0 + (j + 1) * E], (upper if q == j else ones_b)[:],
                                          flat[:, q * E:(q + 1) * E], start=(q == 0), stop=(q == j))
                        for q in range(TPB):
                            ins = pe.matmul(ps[:, 2, CT0:CT0 + E], ones_b[:], flat[:, q * E:(q + 1) * E],
                                            start=(q == 0), stop=(q == TPB - 1))
                    ins.then_inc(R["lg_ps", L], 1)

                turn_x(0)
                turn_ctx(0)
                project_q(0)
                project_kv(0)
                scores(0, 0)
                scores(0, 1)
                pe.wait_ge(late_loaded, late_there[L])
                if L == 1:
                    turn_x(1)
                    turn_ctx(1)
                    project_q(1)
                    project_kv(1)

                def batch0(b, _r, _m):
                    nxt, past = before(b, NB - 1), not isinstance(b, int) or b > 0
                    turn_p(b, 0)
                    scores(b, 2)
                    if past:
                        turn_attn(b - 1, 1)
                    weigh_v(b, 0)
                    if past:
                        project_out(b - 1, 1)
                    turn_p(b, 1)
                    if since(b, 2):
                        route(b - 2)
                    if nxt:
                        turn_x(b + 1)
                    scores(b, 3)
                    if nxt:
                        turn_ctx(b + 1)
                    weigh_v(b, 1)
                    if nxt:
                        project_q(b + 1)
                    turn_p(b, 2)
                    if nxt:
                        project_kv(b + 1)
                    weigh_v(b, 2)
                    if nxt:
                        scores(b + 1, 0)
                    turn_attn(b, 0)
                    turn_p(b, 3)
                    if nxt:
                        scores(b + 1, 1)
                    project_out(b, 0)
                    weigh_v(b, 3)
                    if past:
                        turn_rows(b - 1)

                def batch1(b, _r, _m):
                    turn_p(b, 0)
                    if since(b, 2):
                        turn_rows(b - 2)
                    if before(b, NB - 1):
                        scores(b + 1, 0)
                    weigh_v(b, 0)
                    if since(b, 2):
                        route(b - 2)
                    if before(b, NB - 2):
                        turn_x(b + 2)
                    turn_p(b, 1)
                    if before(b, NB - 2):
                        turn_ctx(b + 2)
                    if before(b, NB - 1):
                        scores(b + 1, 1)
                    if before(b, NB - 2):
                        project_q(b + 2)
                    weigh_v(b, 1)
                    if before(b, NB - 2):
                        project_kv(b + 2)

                if L == 0:
                    loop(pe, NB, batch0, head=3)
                    turn_attn(NB - 1, 1)
                    project_out(NB - 1, 1)
                    route(NB - 2)
                else:
                    loop(pe, NB, batch1, head=3, tail=2)
                    turn_rows(NB - 2)
                    route(NB - 2)
                turn_rows(NB - 1)
                route(NB - 1)
                route(NB)

                I, CW = FFN[L]["I"], FFN[L]["CW"]
                NCH, KC = I // CW, I // P
                pe.wait_ge(weights_loaded[L], 16 * 2 * NB)
                pe.wait_ge(bias_split, L + 1)
                pe.wait_ge(R["routed", L], 1)

                def f_turn(i):
                    pe.wait_ge(F["x_done", L], i + 1)
                    wait(pe, F["xT_sb", L], i)
                    for c in range(NC):
                        ins = pe.transpose(ps[:, 5, c * P:(c + 1) * P], f_xn[:, c * P:(c + 1) * P], ident[:])
                    ins.then_inc(F["xT_ps", L], 1)

                def expert_of(i):
                    return pe.value_load(tile_expert[0:1, bass.ds(i, 1)], min_val=0, max_val=E - 1)

                def flat(ap):
                    return ap.rearrange("p a b -> p (a b)")

                def hidden(i, n, e):
                    if n == 0:
                        pe.wait_ge(F["xT_sb", L], i + 1)
                    wait(pe, F["h_sb", L], NCH * (i - 1) + n + 1)
                    pe.matmul(ps[:, n, 0:CW], flat(expert_rows[:, bass.ds(e, 1), :]), biasw[:, n * CW:(n + 1) * CW],
                              start=True, stop=False)
                    for k in range(NC):
                        ins = pe.matmul(ps[:, n, 0:CW], f_xT[:, k, :], flat(w1sb[:, bass.ds(e * NC + k, 1), n * CW:(n + 1) * CW]),
                                        start=False, stop=(k == NC - 1))
                    ins.then_inc(F["h_ps", L], 1)

                def turn_h(i, n):
                    pe.wait_ge(F["h_sb", L], NCH * i + n + 1)
                    wait(pe, F["hT_sb", L], NCH * (i - 1) + n + 1)
                    for q in range(CW // P):
                        ins = pe.transpose(ps[:, 2 + n, q * P:(q + 1) * P], f_h[:, n * CW + q * P:n * CW + (q + 1) * P], ident[:])
                    ins.then_inc(F["hT_ps", L], 1)

                def down(i, e):
                    wait(pe, F["y_sb", L], i)
                    pe.matmul(ps[:, 6, 0:D], flat(expert_rows[:, bass.ds(e, 1), :]), biasw[:, I:I + D], start=True, stop=False)
                    for k in range(KC):
                        if k % (CW // P) == 0:
                            pe.wait_ge(F["hT_sb", L], NCH * i + k // (CW // P) + 1)
                        ins = pe.matmul(ps[:, 6, 0:D], f_hT[:, k, :], flat(w2sb[:, bass.ds(e * KC + k, 1), :]),
                                        start=False, stop=(k == KC - 1))
                    ins.then_inc(F["y_ps", L], 1)

                f_turn(0)
                e0 = expert_of(0)
                for n in range(NCH):
                    hidden(0, n, e0)
                f_turn(1)

                def tile(i, _r, _m):
                    nxt = not isinstance(i, int) or i + 1 < SLOT_TILES
                    if nxt:
                        e_next = expert_of(i + 1)
                        if NCH == 2:
                            hidden(i + 1, 0, e_next)
                    for n in range(NCH):
                        turn_h(i, n)
                    if nxt and NCH == 2:
                        hidden(i + 1, 1, e_next)
                    if before(i, SLOT_TILES - 2):
                        f_turn(i + 2)
                    if nxt and NCH == 1:
                        hidden(i + 1, 0, e_next)
                    down(i, expert_of(i))

                loop(pe, SLOT_TILES, tile, unroll=3)

        @block.vector
        def _(dve):
            def split_bias(L):
                n = FFN[L]["I"] + D
                f = biasf[L][:, 0:n]
                dve.wait_ge(bias_loaded, 16 * 6 * (L + 1))
                w = biasw[:, 0:n]
                ch = Chain(dve, bias_link)
                ch.begin(4 * L)
                link = ch.link
                link(dve.tensor_copy(w, f))
                link(dve.tensor_tensor(f, f, w, ALU.subtract))
                dve.tensor_copy(w[32:64], f[32:64])
                link(dve.tensor_copy(w[64:96], f[64:96]))
                link(dve.tensor_tensor(f[64:96], f[64:96], w[64:96], ALU.subtract))
                dve.tensor_copy(w[64:96], f[64:96]).then_inc(bias_split, L + 1)

            dve.memset(biasf[0][:, 0:FFN[0]["I"] + D], 0.0).then_inc(bias_zeroed, 1)
            for L in (0, 1):
                U, H, hpc = (ATT[L][k] for k in ("units", "H", "hpc"))
                d = D // H
                prep = Chain(dve, A["prep_chain", L], wait_carried)
                sm_chain, norm_chain = Chain(dve, A["sm_chain", L]), Chain(dve, norm_link)
                sm_links = (2, 2, 1, 1) if L == 0 else (2, 2)
                hm = headmask[L]

                def row(t):
                    return xres[:, bass.ds(t, 1), 0:D].rearrange("p a d -> p (a d)")

                def prep_stats(b):
                    prep.begin(b)
                    dve.wait_ge(A["x_loaded", L], 16 * b + 16)
                    wait(dve, A["xhat_done", L], b)
                    dve.sem_inc(wait_carried, 1)
                    for j in range(TPB):
                        ins = dve.bn_stats(xst[:, j, :], row(TPB * b + j))
                    prep.link(ins)
                    for j in range(TPB):
                        ins = dve.bn_aggr(mv[:, j, :], xst[:, j, :])
                    ins.then_inc(A["stats_done", L], 1)

                def prep_apply(b):
                    dve.wait_ge(A["rstd_done", L], b + 1)
                    wait(dve, A["xT_ps", L], b)
                    for j in range(TPB):
                        ins = dve.tensor_scalar(xhat[:, j, :], row(TPB * b + j), mv[:, j, 0:1], rstd[:, j:j + 1],
                                                ALU.subtract, ALU.mult)
                    ins.then_inc(A["xhat_done", L], 1)

                def scale_mask(b):
                    dve.wait_ge(A["mask_loaded", 1], 16 * b + 16)
                    dve.tensor_scalar(maskneg[:], rawmask, -ATT[1]["mask_val"], None, ALU.mult).then_inc(A["mask_done", 1], 1)

                def make_kbd(b):
                    dve.wait_ge(A["kv_ps", L], b + 1)
                    wait(dve, A["s_ps", L], U * b)
                    for c in range(NC):
                        ins = dve.scalar_tensor_tensor(
                            out=kbd[:, c, 0:hpc * Z].rearrange("p (h z) -> p h z", h=hpc),
                            in0=ps[:, 7, c * Z:(c + 1) * Z].unsqueeze(1).broadcast_to([P, hpc, Z]), scalar=bk[:, c:c + 1],
                            in1=hm[:].unsqueeze(2).broadcast_to([P, hpc, Z]), op0=ALU.add, op1=ALU.mult)
                    ins.then_inc(A["kbd_done", L], 1)

                def make_v(b):
                    wait(dve, A["v_done", L], b)
                    dve.tensor_tensor(vnext[:, 0:H * (d + 1)].rearrange("p (h e) -> p h e", h=H)[:, :, 0:d],
                                      ps[0:Z, 7, D:2 * D].rearrange("p (h e) -> p h e", h=H),
                                      bv[:].rearrange("p (h e) -> p h e", h=H), ALU.add).then_inc(A["v_evac", L], 1)

                def softmax_unit(b, u):
                    n, buf = U * b + u, u % 2
                    sm_chain.begin(sum(sm_links) * b + sum(sm_links[:u]))
                    dve.wait_ge(A["s_ps", L], n + 1)
                    wait(dve, A["pt_ps", L], 2 * (n - 1))
                    src = ps[:, 2 * buf:2 * buf + 2, 0:GZ].rearrange("p g (k z) -> p g k z", k=HG)
                    dst = p_sb[buf].rearrange("p g (k z) -> p g k z", k=HG)
                    j = u // 2 if L == 0 else u
                    if sm_links[u] == 2:
                        if L == 1 and u == 0:
                            dve.wait_ge(A["mask_done", 1], b + 1)
                        m = maskneg[:, j, :].unsqueeze(1).unsqueeze(1).broadcast_to([P, 2, HG, Z])
                        sm_chain.link(dve.tensor_tensor(dst, src, m, ALU.add))
                        src = dst
                    m8 = mx.rearrange("p (g k) -> p g k", g=2)
                    wait(dve, A["sub_done", L], n)
                    sm_chain.link(dve.tensor_reduce(m8, src, AX, ALU.max))
                    dve.tensor_tensor(dst, src, m8.unsqueeze(3).broadcast_to([P, 2, HG, Z]), ALU.subtract
                                      ).then_inc(A["sub_done", L], 1)

                def normalise(b, j):
                    norm_chain.begin(TPB * (b + NB * L) + j)
                    dve.wait_ge(A["av_ps", L], U * b + (2 * j + 2 if L == 0 else j + 1))
                    av = ps[:, 6, 0:H * (d + 1)].rearrange("p (h e) -> p h e", h=H)
                    wait(dve, A["attn_done", L], TPB * b + j)
                    norm_chain.link(dve.reciprocal(rinv[:, 0:H].unsqueeze(2), av[:, :, d:d + 1]))
                    if L == 0:
                        wait(dve, A["at_ps", 0], TPB * b + j)
                    else:
                        wait(dve, A["res_done", 1], TPB * b + j)
                    ins = dve.tensor_tensor(attn.rearrange("p (h e) -> p h e", h=H), av[:, :, 0:d],
                                            rinv[:, 0:H].unsqueeze(2).broadcast_to([P, H, d]), ALU.mult)
                    ins.then_inc(A["attn_done", L], 1)
                    if L == 1:
                        dve.wait_ge(A["attn_done", 1], TPB * b + j + 1)
                        t = row(TPB * b + j)
                        dve.scalar_tensor_tensor(out=t, in0=attn, scalar=tg[:, 1:2], in1=t, op0=ALU.mult, op1=ALU.add
                                                 ).then_inc(A["res_done", 1], 1)

                def residual(b, j):
                    dve.wait_ge(A["wo_ps", L], TPB * b + j + 1)
                    t = row(TPB * b + j)
                    dve.scalar_tensor_tensor(out=t, in0=ps[:, 7, 0:D], scalar=tg[:, 0:1], in1=t, op0=ALU.mult, op1=ALU.add
                                             ).then_inc(A["res_done", L], 1)

                rch = Chain(dve, rows_link, wait_carried)
                ch = Chain(dve, R["route_chain", L])
                route_links = 7 if L == 0 else 5

                def row_stats(k):
                    rch.begin(k + NB * L)
                    wait(dve, R["x_done", L], k)
                    if L == 0:
                        dve.wait_ge(A["bo_done", 0], TPB * k + TPB)
                    else:
                        dve.wait_ge(A["res_done", 1], TPB * k + TPB)
                    dve.sem_inc(wait_carried, 1)
                    for j in range(TPB):
                        ins = dve.bn_stats(r_st[:, j, :], row(TPB * k + j))
                    rch.link(ins)
                    for j in range(TPB):
                        ins = dve.bn_aggr(r_mv[:, j, :], r_st[:, j, :])
                    ins.then_inc(R["stats_done", L], 1)

                def row_apply(k):
                    dve.wait_ge(R["rstd_done", L], k + 1)
                    wait(dve, R["xT_ps", L], k)
                    for j in range(TPB):
                        ins = dve.tensor_scalar(r_x[:, j, :], row(TPB * k + j), r_mv[:, j, 0:1], r_rstd[:, j:j + 1],
                                                ALU.subtract, ALU.mult)
                    ins.then_inc(R["x_done", L], 1)

                def over_e(ap):
                    return ap.unsqueeze(2).broadcast_to([P, TPB, E])

                def over_t(ap):
                    return ap.unsqueeze(1).broadcast_to([P, TPB, E])

                def bank2(at, n):
                    return ps[:, 2, at:at + n]

                def choose(k):
                    new, old = before(k, NB), since(k, 1)
                    ch.begin(route_links * k)
                    dve.wait_ge(R["lg_ps", L], k + 1)
                    if new:
                        ins = dve.tensor_tensor(lg, bank2(LG0, TPB * E).rearrange("p (t e) -> p t e", e=E), over_t(brb[:]), ALU.add)
                    if old:
                        ins = dve.tensor_tensor(slot_of, bank2(RK0, TPB * E).rearrange("p (t e) -> p t e", e=E), over_t(row_base[:]), ALU.add)
                        ch.link(ins)
                        dve.tensor_tensor(row_base[:], row_base[:], bank2(CT0, E), ALU.add).then_inc(R["lg_done", L], 1)
                        if L == 0:
                            dve.wait_ge(R["gate_exp", 0], k)
                            dve.tensor_scalar(gate_new[:], gate_new[:], 1.0, None, ALU.add)
                        ins = dve.tensor_tensor(slot_of, slot_of, one_hot[:], ALU.mult)
                    else:
                        ins.then_inc(R["lg_done", L], 1)
                        dve.wait_ge(R["lg_done", L], 1)
                        ch.link(dve.memset(slot_of, 0.0))
                    if new:
                        ins = dve.tensor_reduce(tmax, lg, AX, ALU.max)
                    ch.link(ins)
                    if old:
                        if L == 0:
                            dve.reciprocal(gate_new[:], gate_new[:])
                        ins = dve.tensor_reduce(slot_f, slot_of, AX, ALU.add)
                    if new:
                        ins = dve.tensor_tensor(is_top, lg, over_e(tmax), ALU.is_equal)
                    ch.link(ins)
                    if L == 0 and old:
                        dve.tensor_scalar(xres[:, bass.ds(TPB * (k - 1), TPB), D], gate_new[:], tg[:, 2:3], None, ALU.mult)
                    if old:
                        dve.tensor_copy(slot_i[:, bass.ds(TPB * (k - 1), TPB)], slot_f).then_inc(R["slot_done", L], 1)
                    if not new:
                        return
                    ch.link(dve.tensor_tensor(is_top, is_top, over_t(exp_rev[:]), ALU.mult))
                    ch.link(dve.tensor_reduce(tmax2, is_top, AX, ALU.max))
                    dve.tensor_tensor(one_hot[:], is_top, over_e(tmax2), ALU.is_equal).then_inc(R["onehot_done", L], 1)
                    if L == 0:
                        dve.wait_ge(R["onehot_done", L], k + 1)
                        ch.link(dve.scalar_tensor_tensor(out=is_top, in0=one_hot[:], scalar=-3.0e38, in1=lg, op0=ALU.mult, op1=ALU.add))
                        ch.link(dve.tensor_reduce(tmax2, is_top, AX, ALU.max))
                        dve.tensor_tensor(gate_new[:], tmax2, tmax, ALU.subtract).then_inc(R["gap_done", 0], 1)

                if L == 0:
                    dve.wait_ge(const_made, 2)
                else:
                    rows_back(dve, 0)
                    dve.memset(biasf[1], 0.0).then_inc(bias_zeroed, 1)
                dve.memset(vnext, 1.0).then_inc(vaug_ones, 1)
                dve.wait_ge(vaug_ones, L + 1)
                prep_stats(0)
                prep_apply(0)
                if L == 1:
                    scale_mask(0)
                    prep_stats(1)
                    prep_apply(1)
                dve.wait_ge(const_loaded, consts_there[L])
                make_kbd(0)
                make_v(0)
                softmax_unit(0, 0)
                if L == 1:
                    softmax_unit(0, 1)
                    scale_mask(1)
                    prep_stats(2)
                    make_kbd(1)
                    make_v(1)
                split_bias(L)

                def batch0(b, _r, _m):
                    nxt, past = before(b, NB - 1), not isinstance(b, int) or b > 0
                    softmax_unit(b, 1)
                    softmax_unit(b, 2)
                    if nxt:
                        prep_apply(b + 1)
                    if past:
                        residual(b - 1, 1)
                    softmax_unit(b, 3)
                    normalise(b, 0)
                    if past:
                        row_stats(b - 1)
                    if since(b, 2):
                        choose(b - 2)
                    if nxt:
                        make_kbd(b + 1)
                        make_v(b + 1)
                        softmax_unit(b + 1, 0)
                    if before(b, NB - 2):
                        prep_stats(b + 2)
                    residual(b, 0)
                    if past:
                        row_apply(b - 1)
                    normalise(b, 1)

                def batch1(b, _r, _m):
                    if before(b, NB - 2):
                        prep_apply(b + 2)
                    if before(b, NB - 1):
                        softmax_unit(b + 1, 0)
                    if since(b, 1):
                        row_stats(b - 1)
                    normalise(b, 0)
                    if before(b, NB - 1):
                        softmax_unit(b + 1, 1)
                    if since(b, 1):
                        row_apply(b - 1)
                    if before(b, NB - 2):
                        scale_mask(b + 2)
                    if before(b, NB - 3):
                        prep_stats(b + 3)
                    if before(b, NB - 2):
                        make_kbd(b + 2)
                        make_v(b + 2)
                    normalise(b, 1)
                    if since(b, 2):
                        choose(b - 2)

                if L == 0:
                    dve.wait_ge(tanh_done, 1)
                    prep_stats(1)
                    loop(dve, NB, batch0, head=3, tail=2)
                    residual(NB - 1, 1)
                else:
                    loop(dve, NB, batch1, head=3, tail=3)

                row_stats(NB - 1)
                row_apply(NB - 1)
                choose(NB - 2)
                choose(NB - 1)
                choose(NB)
                dve.wait_ge(R["lg_done", L], NB + 1)
                dve.wait_ge(R["slot_done", L], NB)
                link = ch.link
                dve.tensor_copy(pad_row[:], row_base[0:1]).then_inc(R["pads_known", L], 1)
                dve.memset(ones8, 1.0)
                link(dve.tensor_tensor(total, row_base[:], region0[:], ALU.subtract))
                link(dve.tensor_tensor(steps_below, total.unsqueeze(2).broadcast_to([P, E, NT]),
                                       steps128[:].unsqueeze(1).broadcast_to([P, E, NT]), ALU.is_gt))
                link(dve.tensor_reduce(tiles, steps_below, AX, ALU.add))
                link(dve.tensor_tensor_scan(tend, ones8, tiles, 0.0, ALU.mult, ALU.add))
                dve.tensor_scalar(delta, tiles, -float(P), float(REGION), ALU.mult, ALU.add)
                link(dve.tensor_tensor(te_cmp, tile_no[:].unsqueeze(2).broadcast_to([1, 40, E]),
                                       tend[0:1].unsqueeze(1).broadcast_to([1, 40, E]), ALU.is_ge))
                dve.tensor_reduce(te_sum, te_cmp, AX, ALU.add)
                link(dve.scalar_tensor_tensor(out=delta[:, E - 1:E], in0=tend[:, E - 1:E], scalar=float(P),
                                              in1=delta[:, E - 1:E], op0=ALU.mult, op1=ALU.add))
                dve.tensor_scalar(tile_expert[:], te_sum, float(E - 1), None, ALU.min)
                link(dve.tensor_scalar(delta[:, E - 1:E], delta[:, E - 1:E], -float(MIN_TILES * P), None, ALU.add))
                link(dve.tensor_tensor(te_cmp, te_cmp, delta[0:1].unsqueeze(1).broadcast_to([1, 40, E]), ALU.mult))
                link(dve.tensor_reduce(te_sum, te_cmp, AX, ALU.add))
                link(dve.scalar_tensor_tensor(out=tile_row[:], in0=tile_no[:], scalar=float(P), in1=te_sum, op0=ALU.mult,
                                              op1=ALU.add))
                dve.tensor_copy(row_base[:], region0[:]).then_inc(R["routed", L], 1)

                I, CW = FFN[L]["I"], FFN[L]["CW"]
                NCH = I // CW
                fch = Chain(dve, experts_link, wait_carried)

                def f_stats(i, r, m):
                    fch.begin(i + SLOT_TILES * L)
                    wait(dve, F["x_done", L], i)
                    dve.wait_ge(xs_loaded[r], 16 * (m + 1 + uses(r) * L))
                    dve.sem_inc(wait_carried, 1)
                    fch.link(dve.bn_stats(f_st, xs[r][:, 0:D]))
                    dve.bn_aggr(f_mv, f_st).then_inc(F["stats_done", L], 1)

                def f_apply(i, r):
                    dve.wait_ge(F["rstd_done", L], i + 1)
                    wait(dve, F["xT_ps", L], i)
                    dve.tensor_scalar(f_xn, xs[r][:, 0:D], f_mv[:, 0:1], f_rstd, ALU.subtract, ALU.mult).then_inc(F["x_done", L], 1)

                def xT_evac(i):
                    dve.wait_ge(F["xT_ps", L], i + 1)
                    wait(dve, F["h_ps", L], NCH * i)
                    dve.tensor_copy(f_xT.rearrange("p a b -> p (a b)"), ps[:, 5, 0:D]).then_inc(F["xT_sb", L], 1)

                def hT_evac(i, n):
                    q = CW // P
                    dve.wait_ge(F["hT_ps", L], NCH * i + n + 1)
                    wait(dve, F["y_ps", L], i)
                    dve.tensor_copy(f_hT[:, n * q:(n + 1) * q, :].rearrange("p a b -> p (a b)"), ps[:, 2 + n, 0:CW]
                                    ).then_inc(F["hT_sb", L], 1)

                def finish(i, r, m):
                    wait(dve, y_scattered[r], 16 * (m + uses(r) * L))
                    dve.tensor_copy(token_i[:, r:r + 1], xs[r][:, D + 1:ROW])
                    dve.wait_ge(F["y_ps", L], i + 1)
                    dve.scalar_tensor_tensor(out=f_y[r], in0=ps[:, 6, 0:D], scalar=xs[r][:, D:D + 1] if L == 0 else tg[:, 3:4],
                                             in1=xs[r][:, 0:D], op0=ALU.mult, op1=ALU.add).then_inc(F["y_sb", L], 1)

                for i in range(3):
                    f_stats(i, i, 0)
                    f_apply(i, i)
                    if i < 2:
                        xT_evac(i)

                def tile(i, r, m):
                    for n in range(NCH):
                        hT_evac(i, n)
                    nxt, nm = (r + 3) % RING, m + (r + 3) // RING
                    if before(i, SLOT_TILES - 3):
                        f_stats(i + 3, nxt, nm)
                    if before(i, SLOT_TILES - 2):
                        xT_evac(i + 2)
                    if before(i, SLOT_TILES - 3):
                        f_apply(i + 3, nxt)
                    finish(i, r, m)

                loop(dve, SLOT_TILES, tile, unroll=RING, tail=0)


_INS = ['x', 'ctx_1024', 'mask_BxSxS2_ff0', 'g_xattn', 'g_ffn', 'L0_xattn_w_q', 'L0_xattn_b_q', 'L0_xattn_w_kv',
        'L0_xattn_b_kv', 'L0_xattn_w_out', 'L0_xattn_b_out', 'L0_ffn_w1', 'L0_ffn_b1', 'L0_ffn_w2', 'L0_ffn_b2',
        'L0_ffn_wr', 'L0_ffn_br', 'L1_xattn_wq_kernel', 'L1_xattn_wq_bias', 'L1_xattn_wk_kernel', 'L1_xattn_wk_bias',
        'L1_xattn_wv_kernel', 'L1_xattn_wv_bias', 'L1_ffn_Wg', 'L1_ffn_bg', 'L1_ffn_W1', 'L1_ffn_b1', 'L1_ffn_W2',
        'L1_ffn_b2']


def kernel(**inputs):
    import numpy as _np
    import concourse.bacc as _bacc
    from concourse import mybir as _mybir
    from concourse.bass_utils import run_bass_kernel_spmd as _run

    nc = _bacc.Bacc("TRN2", target_bir_lowering=False, num_devices=1)
    arrays, args = {}, []
    for name in _INS:
        a = _np.ascontiguousarray(inputs[name])
        arrays[f"in_{name}_dram"] = a
        args.append(nc.dram_tensor(f"in_{name}_dram", a.shape, _mybir.dt.from_np(a.dtype), kind="ExternalInput").ap())
    args.append(nc.dram_tensor("out_0_dram", (NB, S, D), _mybir.dt.float32, kind="ExternalOutput").ap())
    flamingo_kernel(nc, *args)
    r = _run(nc, [arrays], core_ids=[0])
    return r.results[0]["out_0_dram"]
```

```python
from contextlib import ExitStack

import concourse.bass as bass
from concourse import mybir

ALU = mybir.AluOpType
ACT = mybir.ActivationFunctionType
F32 = mybir.dt.float32
BF16 = mybir.dt.bfloat16
I32 = mybir.dt.int32
AX = mybir.AxisListType.X

P = 128
NB, S, D, Z = 16, 256, 256, 77
NC = D // P
TPB = S // P
NT = NB * TPB
E = 8
SLOT_TILES = (NB * S + E * (P - 1)) // P
REGION = NB * S + P
MIN_TILES = NB * S // P
NROWS = E * REGION + (SLOT_TILES - MIN_TILES) * P
EPS = 1e-5
RING = 6
ROW = D + 2
HG = 4
GZ = HG * Z
LG0 = GZ
RK0 = LG0 + TPB * E
CT0 = RK0 + TPB * E

ATT = {
    0: dict(H=16, hpc=8, units=4, mask_val=1e12),
    1: dict(H=8, hpc=4, units=2, mask_val=1e9),
}
HIDDEN = {0: 1024, 1: 256}
H_RING = 3


def wait(eng, sem, value):
    if isinstance(value, int) and value <= 0:
        return
    eng.wait_ge(sem, value)


class Chain:

    def __init__(self, eng, sem, apart=None):
        self.eng, self.sem, self.apart = eng, sem, apart

    def begin(self, before):
        self.made = before

    def link(self, ins):
        self.made = self.made + 1
        ins.then_inc(self.sem, 1)
        self.eng.wait_ge(self.sem, self.made)
        if self.apart is not None:
            self.eng.sem_inc(self.apart, 1)


def loop(eng, n, step, unroll=1, head=1, tail=1):
    for i in range(head * unroll):
        step(i, i % unroll, i // unroll)
    end = n // unroll - tail
    with eng.Fori(head, end) as m:
        for r in range(unroll):
            step(m * unroll + r, r, m)
    for i in range(end * unroll, n):
        step(i, i % unroll, i // unroll)


def before(i, n):
    return not isinstance(i, int) or i < n


def since(i, n):
    return not isinstance(i, int) or i >= n


def upto(i, n):
    return min(i, n) if isinstance(i, int) else i


def flamingo_kernel(nc, x, ctx_in, mask, g_xattn, g_ffn,
                    w_q0, b_q0, w_kv0, b_kv0, w_o0, b_o0, w1_0, b1_0, w2_0, b2_0, wr0, br0,
                    w_q1, b_q1, w_k1, b_k1, w_v1, b_v1, wr1, br1, w1_1, b1_1, w2_1, b2_1, out):
    with ExitStack() as ctx:
        def sb(name, shape, dt=F32):
            return ctx.enter_context(nc.sbuf_tensor(name, shape, dt))

        def sem(name):
            return ctx.enter_context(nc.semaphore(name))

        slots_dram = nc.dram_tensor("slot_rows", (NROWS, ROW), F32, kind="Internal").ap()
        xmid_dram = nc.dram_tensor("x_between_layers", (NB * S, D), F32, kind="Internal").ap()

        xres = sb("xres", [P, NT, ROW])
        w1sb = sb("w1sb", [P, E * NC, 1024])
        w2sb = sb("w2sb", [P, E * 8, D])
        wq, wk, wv, wo = (sb(n, [P, NC, D]) for n in ("wq", "wk", "wv", "wo"))
        bq, bk = sb("bq", [P, NC]), sb("bk", [P, NC])
        bv = sb("bv", [Z, D])
        tg = sb("tg", [P, 4])
        ident = sb("ident", [P, P])
        headmask = {0: sb("headmask0", [P, 8]), 1: sb("headmask1", [P, 4])}
        maskneg = sb("maskneg", [P, TPB, Z])
        wr = sb("wr", [P, NC, E])
        brb = sb("brb", [P, E])
        gate_new = sb("gate_new", [P, TPB])
        slot_i = sb("slot_i", [P, NT], I32)
        tile_expert = sb("tile_expert", [1, 40], I32)
        tile_row = sb("tile_row", [1, 40], I32)
        pad_row = sb("pad_row", [1, E], I32)
        expert_rows = sb("expert_rows", [96, E, P], BF16)
        b2w = sb("b2w", [96, D], BF16)
        b1T = sb("b1T", [P, 8, E])
        halfneg = sb("halfneg", [P, TPB])
        eps = sb("eps", [P, TPB])
        gated_bo = sb("gated_bo", [P, D])
        pad_rows = sb("pad_rows", [P, ROW])
        token_f, token_i = sb("token_f", [P, 1]), sb("token_i", [P, RING], I32)

        SCRATCH = 7184
        scratch = sb("scratch", [P, SCRATCH])

        def carve(*shapes):
            at, got = 0, []
            for shape in shapes:
                n = 1
                for s in shape[1:]:
                    n *= s
                ap = scratch[0:shape[0], at:at + n]
                if len(shape) == 3:
                    ap = ap.rearrange("p (a b) -> p a b", a=shape[1])
                got.append(ap)
                at += n
            assert at <= SCRATCH, at
            return got

        (xhat, xT, ctxs, cT, qT, kbd, vaug, vnext, p0, p1, pt0, pt1, attn, attnT, xst, mv, veps, rstd, mx, rinv,
         r_x, r_st, r_mv, r_veps, r_rstd, lg, is_top, slot_of, tmax, tmax2, slot_f
         ) = carve([P, TPB, D], [P, NC, S], [Z, D], [P, NC, Z], [P, NC, S], [P, NC, 8 * Z], [Z, 16 * 17], [Z, 16 * 17],
                   [P, 2, GZ], [P, 2, GZ], [Z, HG, P], [Z, HG, P], [P, D], [P, NC, P],
                   [P, TPB, 6], [P, TPB, 2], [P, TPB], [P, TPB], [P, 2 * HG], [P, 16],
                   [P, TPB, D], [P, TPB, 6], [P, TPB, 2], [P, TPB], [P, TPB], [P, TPB, E], [P, TPB, E], [P, TPB, E],
                   [P, TPB], [P, TPB], [P, TPB])
        p_sb, pt_sb = [p0, p1], [pt0, pt1]
        rawmask = attnT.rearrange("p a b -> p (a b)")[:, 0:TPB * Z].rearrange("p (a b) -> p a b", a=TPB)
        r_flat = r_x.rearrange("p a b -> p (a b)")
        steps_below = r_flat[:, 0:NT * E].rearrange("p (a b) -> p a b", a=E)
        te_cmp = r_flat[0:1, 0:40 * E].rearrange("p (a b) -> p a b", a=40)
        te_sum = r_flat[0:1, 40 * E:40 * E + 40]
        total, tiles, tend, ones8, delta = (r_flat[:, 40 * (E + 1) + q * E:40 * (E + 1) + (q + 1) * E] for q in range(5))
        one_hot = sb("one_hot", [P, TPB, E], BF16)
        row_base = sb("row_base", [P, E])
        region0 = sb("region0", [P, E])
        upper = sb("upper", [P, P], BF16)
        ones_b = sb("ones_b", [P, P], BF16)
        exp_rev = sb("exp_rev", [P, E])
        steps128 = sb("steps128", [P, NT])
        tile_no = sb("tile_no", [1, 40])
        (f_xn, f_xT, w1_tile, f_hT, f_st, f_mv, f_veps, f_rstd, *f_rows
         ) = carve([P, D], [P, NC, P], [P, NC, 1024], [P, 8, P], [P, 6], [P, 2], [P, 1], [P, 1], *[[P, ROW]] * RING, *[[P, D]] * RING)
        xs, f_y = f_rows[0:RING], f_rows[RING:]
        b1_rows = {0: w1sb[0:E, 14, :], 1: w1sb[0:E, 0, D:2 * D]}
        b2_rows = {0: w1sb[0:96, 15, 0:D], 1: w1sb[0:96, 0, 2 * D:3 * D]}

        ps = ctx.enter_context(nc.psum_tensor("ps", [P, 8, 512], F32))

        const_loaded = sem("const_loaded")
        late_loaded = sem("late_loaded")
        const_made, const_chain, tanh_done, tgb_done = sem("const_made"), sem("const_chain"), sem("tanh_done"), sem("tgb_done")
        zeros_made, zero_stored, weights_loaded = sem("zeros_made"), sem("zero_stored"), {0: sem("weights_loaded0"), 1: sem("weights_loaded1")}
        a_rstd_chain, r_rstd_chain, f_rstd_chain, norm_link, rows_link, experts_link = (
            sem(n) for n in ("a_rstd_chain", "r_rstd_chain", "f_rstd_chain", "norm_link", "rows_link", "experts_link"))
        A = {}
        for L in (0, 1):
            for n in ("x_loaded", "ctx_loaded", "mask_loaded", "stats_done", "rstd_done", "xhat_done",
                      "prep_chain", "sm_chain", "xT_ps", "xT_sb", "cT_ps", "cT_sb", "q_ps", "q_sb", "kv_ps", "kbd_done",
                      "v_evac", "v_done", "mask_done", "s_ps", "sub_done", "exp_done", "pt_ps", "pt_sb", "av_ps", "attn_done", "at_ps", "at_sb",
                      "wo_ps", "res_done", "bo_done"):
                if L == 0 and n.startswith("mask") or L == 1 and n in ("at_ps", "at_sb", "wo_ps", "bo_done"):
                    continue
                A[n, L] = sem(f"a{L}_{n}")
        R = {(n, L): sem(f"r{L}_{n}") for L in (0, 1) for n in (
            "stats_done", "rstd_done", "x_done", "xT_ps", "xT_sb", "lg_ps", "lg_done", "onehot_done",
            "slot_done", "gap_done", "gate_exp", "route_chain", "pads_known", "routed", "scattered", "pads_stored")
             if L == 0 or n not in ("gap_done", "gate_exp")}
        F = {(n, L): sem(f"f{L}_{n}") for L in (0, 1) for n in (
            ["stats_done", "rstd_done", "x_done", "xT_ps", "xT_sb", "w1a_done", "w1b_done", "h_ps", "hT_sb",
             "y_ps", "y_sb"])}
        xs_loaded = [sem(f"xs_loaded{r}") for r in range(RING)]
        y_scattered = [sem(f"y_scattered{r}") for r in range(RING)]
        bias_zeroed, bias_loaded, bias_split, bias_link, vaug_ones = (
            sem(n) for n in ("bias_zeroed", "bias_loaded", "bias_split", "bias_link", "vaug_ones"))
        bq_done, b1_turned = sem("bq_done"), sem("b1_turned")
        wait_carried, pool_wait_carried = sem("wait_carried"), sem("pool_wait_carried")
        tokens_done = sem("tokens_done")

        def uses(r):
            return (SLOT_TILES - r + RING - 1) // RING

        def rows_back(eng, L):
            for r in range(RING):
                eng.wait_ge(y_scattered[r], 16 * uses(r) * (L + 1))


        consts_there, late_there = {0: 16 * 6, 1: 16 * 12}, {0: 16 * 6, 1: 16 * 8}

        def store_pads(eng, L, experts):
            for e in experts:
                r = eng.value_load(pad_row[0:1, e:e + 1], min_val=0, max_val=E * REGION - P)
                eng.dma_start(slots_dram[bass.ds(r, P), :], pad_rows[:]).then_inc(R["pads_stored", L], 16)

        block = ctx.enter_context(nc.Block())

        @block.sync
        def _(sp):
            def rows(w):
                return w.rearrange("(c p) n -> p c n", p=P)

            def cols(b):
                return b.rearrange("(c p) -> p c", p=P)

            def load_ctx(L, b):
                wait(sp, A["cT_ps", L], b)
                sp.dma_start(ctxs, ctx_in[bass.ds(b, 1), :, :].rearrange("a z d -> (a z) d")).then_inc(A["ctx_loaded", L], 16)

            def load_batch(L, b, with_ctx=True):
                wait(sp, A["x_loaded", L], 16 * b)
                src = x if L == 0 else xmid_dram.rearrange("(b s) d -> b s d", b=NB)
                sp.dma_start(xres[:, bass.ds(TPB * b, TPB), 0:D],
                             src[bass.ds(b, 1), :, :].rearrange("a (j p) d -> p (a j) d", p=P)).then_inc(A["x_loaded", L], 16)
                if with_ctx:
                    load_ctx(L, b)
                if L == 1:
                    wait(sp, A["mask_done", L], b)
                    sp.dma_start(rawmask, mask[bass.ds(b, 1), :, :].rearrange("a (j p) z -> p (a j) z", p=P)
                                 ).then_inc(A["mask_loaded", L], 16)

            def load_consts(L):
                q, late = const_loaded, late_loaded
                wk_src, wv_src = (w_kv0[:, 0:D], w_kv0[:, D:2 * D]) if L == 0 else (w_k1, w_v1)
                sp.dma_start(wk[:], rows(wk_src)).then_inc(q, 16)
                sp.dma_start(wv[:], rows(wv_src)).then_inc(q, 16)
                sp.dma_start(bk[:], cols(b_kv0[0:D] if L == 0 else b_k1), allow_slow_non_contiguous=True).then_inc(q, 16)
                sp.dma_start(bv[:], (b_kv0[D:2 * D] if L == 0 else b_v1).partition_broadcast(Z)).then_inc(q, 16)
                sp.dma_start(wq[:], rows(w_q0 if L == 0 else w_q1)).then_inc(q, 16)
                sp.dma_start(bq[:], cols(b_q0 if L == 0 else b_q1), allow_slow_non_contiguous=True).then_inc(q, 16)
                if L == 0:
                    sp.dma_start(tg[:, 0:2], g_xattn.partition_broadcast(P)).then_inc(late, 16)
                    sp.dma_start(tg[:, 2:4], g_ffn.partition_broadcast(P)).then_inc(late, 16)
                    sp.dma_start(gated_bo[:], b_o0.partition_broadcast(P)).then_inc(late, 16)
                    sp.dma_start(wo[:], rows(w_o0)).then_inc(late, 16)
                sp.dma_start(wr[:], rows(wr0 if L == 0 else wr1)).then_inc(late, 16)
                sp.dma_start(brb[:], (br0 if L == 0 else br1).partition_broadcast(P)).then_inc(late, 16)

            def load_biases(L):
                b1, b2 = (b1_0, b2_0) if L == 0 else (b1_1, b2_1)
                sp.wait_ge(bias_zeroed, L + 1)
                sp.dma_start(b1_rows[L], b1).then_inc(bias_loaded, 16)
                for q in range(3):
                    sp.dma_start(b2_rows[L][32 * q:32 * q + E, :], b2).then_inc(bias_loaded, 16)

            def load_weights(L, b):
                wait(sp, weights_loaded[L], 32 * b)
                if L == 0:
                    sp.dma_start(w1sb[:, bass.ds(b, 1), :],
                                 w1_0.rearrange("e (c p) n -> (e c) p n", p=P)[bass.ds(b, 1), :, :].rearrange("a p n -> p a n")
                                 ).then_inc(weights_loaded[L], 16)
                    sp.dma_start(w2sb[:, bass.ds(4 * b, 4), :],
                                 w2_0.rearrange("e (c p) n -> (e c) p n", p=P)[bass.ds(4 * b, 4), :, :].rearrange("a p n -> p a n")
                                 ).then_inc(weights_loaded[L], 16)
                else:
                    for dst, src in ((w1sb[:, :, 0:D], w1_1), (w2sb, w2_1)):
                        sp.dma_start(dst[:, bass.ds(b, 1), :],
                                     src.rearrange("e (c p) n -> (e c) p n", p=P)[bass.ds(b, 1), :, :].rearrange("a p n -> p a n")
                                     ).then_inc(weights_loaded[L], 16)

            def experts_io(L):
                sp.wait_ge(R["pads_known", L], 1)
                sp.wait_ge(zeros_made, 1)
                store_pads(sp, L, range(0, E, 2))
                sp.wait_ge(R["routed", L], 1)
                sp.wait_ge(R["scattered", L], 16 * NT)
                sp.wait_ge(R["pads_stored", L], 16 * E)
                if L == 0:
                    sp.wait_ge(zero_stored, 16)

                def row_of(i):
                    return bass.ds(sp.value_load(tile_row[0:1, bass.ds(i, 1)], min_val=0, max_val=NROWS - P), P)

                for i in range(RING - 1):
                    sp.dma_start(xs[i][:], slots_dram[row_of(i), :]).then_inc(xs_loaded[i], 16)
                if L == 0:
                    load_consts(1)

                def step(i, r, m):
                    if not isinstance(i, int) or i + RING - 1 < SLOT_TILES:
                        wait(sp, F["y_sb", L], i)
                        nxt = (r + RING - 1) % RING
                        sp.dma_start(xs[nxt][:], slots_dram[row_of(i + RING - 1), :]).then_inc(xs_loaded[nxt], 16)

                loop(sp, SLOT_TILES, step, unroll=RING)

            for L in (0, 1):
                if L == 0:
                    load_ctx(0, 0)
                    load_batch(0, 0, with_ctx=False)
                    load_consts(0)
                else:
                    sp.wait_ge(F["y_sb", 0], SLOT_TILES)
                    load_ctx(1, 0)
                    rows_back(sp, 0)
                    load_batch(1, 0, with_ctx=False)
                load_biases(L)
                load_weights(L, 0)
                with sp.Fori(1, 14) as b:
                    load_batch(L, b)
                    load_weights(L, b)
                sp.wait_ge(bias_split, L + 1)
                for b in (14, 15):
                    load_batch(L, b)
                    load_weights(L, b)
                experts_io(L)

            rows_back(sp, 1)

        @block.gpsimd
        def _(pool):
            c = [0]

            def link(ins):
                c[0] += 1
                ins.then_inc(const_chain, 1)
                pool.wait_ge(const_chain, c[0])

            pool.memset(pad_rows[:, 0:D + 1], 0.0)
            pool.memset(pad_rows[:, D + 1:ROW], float(NB * S)).then_inc(zeros_made, 1)
            pool.iota(token_f[:], pattern=[[0, 1]], base=0, channel_multiplier=1, allow_small_or_imprecise_dtypes=True
                      ).then_inc(tokens_done, 1)
            pool.wait_ge(tokens_done, 1)
            pool.iota(xres[:, :, D + 1], pattern=[[P, NT]], base=0, channel_multiplier=1, allow_small_or_imprecise_dtypes=True)
            for t in (ident, expert_rows, maskneg):
                pool.memset(t[:], 0.0)
            for t in (headmask[0], headmask[1], upper, ones_b):
                pool.memset(t[:], 1.0)
            pool.memset(eps[:], EPS)
            link(pool.memset(halfneg[:], -0.5))
            pool.affine_select(ident[:], ident[:], pattern=[[-1, P]], compare_op=ALU.not_equal, fill=1.0, base=0,
                               channel_multiplier=1)
            for L in (0, 1):
                n, d = ATT[L]["hpc"], P // ATT[L]["hpc"]
                link(pool.affine_select(headmask[L][:], headmask[L][:], pattern=[[-d, n]], compare_op=ALU.is_ge,
                                        fill=0.0, base=0, channel_multiplier=1))
                link(pool.affine_select(headmask[L][:], headmask[L][:], pattern=[[d, n]], compare_op=ALU.is_ge,
                                        fill=0.0, base=d - 1, channel_multiplier=-1))
            pool.affine_select(maskneg[:, 0, :], maskneg[:, 0, :], pattern=[[-1, Z]], compare_op=ALU.is_gt,
                               fill=-ATT[0]["mask_val"], base=0, channel_multiplier=1).then_inc(const_made, 1)
            for q in range(3):
                link(pool.affine_select(expert_rows[:], expert_rows[:], pattern=[[-1, E], [0, P]],
                                        compare_op=ALU.not_equal, fill=1.0, base=-32 * q, channel_multiplier=1))
            pool.affine_select(upper[:], upper[:], pattern=[[1, P]], compare_op=ALU.is_gt, fill=0.0, base=0,
                               channel_multiplier=-1)
            pool.iota(exp_rev[:], pattern=[[-1, E]], base=E, channel_multiplier=0, allow_small_or_imprecise_dtypes=True)
            pool.iota(region0[:], pattern=[[REGION, E]], base=0, channel_multiplier=0, allow_small_or_imprecise_dtypes=True)
            pool.iota(row_base[:], pattern=[[REGION, E]], base=0, channel_multiplier=0, allow_small_or_imprecise_dtypes=True)
            pool.iota(steps128[:], pattern=[[P, NT]], base=0, channel_multiplier=0, allow_small_or_imprecise_dtypes=True)
            pool.iota(tile_no[:], pattern=[[1, 40]], base=0, channel_multiplier=0,
                      allow_small_or_imprecise_dtypes=True).then_inc(const_made, 1)

            def make_rstd(stats_done, chain, past, done, step, var, plus_eps, rs, n):
                pool.wait_ge(stats_done, step + 1)
                pool.tensor_tensor(plus_eps, var, eps[:, 0:n], ALU.add).then_inc(chain, 1)
                pool.wait_ge(chain, past + step + 1)
                pool.tensor_tensor(rs, plus_eps, halfneg[:, 0:n], ALU.pow).then_inc(done, 1)

            for L in (0, 1):
                U = ATT[L]["units"]

                def rstd_batch(b):
                    make_rstd(A["stats_done", L], a_rstd_chain, NB * L, A["rstd_done", L], b, mv[:, :, 1], veps, rstd, TPB)

                def rstd_rows(k):
                    make_rstd(R["stats_done", L], r_rstd_chain, NB * L, R["rstd_done", L], k, r_mv[:, :, 1], r_veps, r_rstd, TPB)

                def scatter(k):
                    pool.wait_ge(R["slot_done", L], k + 1)
                    for t in range(TPB * k, TPB * k + TPB):
                        pool.indirect_dma_start(slots_dram, bass.IndirectOffsetOnAxis(ap=slot_i[:, t:t + 1], axis=0),
                                                xres[:, t, :], None).then_inc(R["scattered", L], 16)

                def add_bias(b, j):
                    pool.wait_ge(A["res_done", 0], TPB * b + j + 1)
                    t = xres[:, bass.ds(TPB * b + j, 1), 0:D].rearrange("p a d -> p (a d)")
                    pool.tensor_tensor(t, t, gated_bo[:], ALU.add).then_inc(A["bo_done", 0], 1)

                def use_v(b):
                    wait(pool, A["av_ps", L], U * b)
                    pool.wait_ge(A["v_evac", L], b + 1)
                    pool.sem_inc(pool_wait_carried, 1)
                    pool.tensor_copy(vaug, vnext).then_inc(A["v_done", L], 1)

                if L == 0:
                    rstd_batch(0)
                    use_v(0)
                    pool.wait_ge(tanh_done, 1)
                    pool.tensor_scalar(gated_bo[:], gated_bo[:], tg[:, 0:1], None, ALU.mult).then_inc(tgb_done, 1)
                    pool.wait_ge(tgb_done, 1)
                    rstd_batch(1)

                    for b in range(NB):
                        if b > 0:
                            add_bias(b - 1, 1)
                            rstd_rows(b - 1)
                        if b > 2:
                            scatter(b - 3)
                        if b < NB - 2:
                            rstd_batch(b + 2)
                        add_bias(b, 0)
                        if b < NB - 1:
                            use_v(b + 1)
                    add_bias(NB - 1, 1)
                else:
                    rstd_batch(0)
                    rstd_batch(1)
                    use_v(0)
                    rstd_batch(2)
                    for b in range(NB):
                        if b > 0:
                            rstd_rows(b - 1)
                        if b + 1 < NB:
                            use_v(b + 1)
                        if b + 3 < NB:
                            rstd_batch(b + 3)
                        if b > 2:
                            scatter(b - 3)

                rstd_rows(NB - 1)
                for k in range(NB - 3, NB):
                    scatter(k)

                def rstd_tile(i):
                    make_rstd(F["stats_done", L], f_rstd_chain, SLOT_TILES * L, F["rstd_done", L], i, f_mv[:, 1:2], f_veps, f_rstd, 1)

                def scatter_tile(i, r, m):
                    if before(i, SLOT_TILES - 4):
                        rstd_tile(i + 4)
                    pool.wait_ge(F["y_sb", L], i + 1)
                    pool.sem_inc(pool_wait_carried, 1)
                    dst = xmid_dram if L == 0 else out.rearrange("b s d -> (b s) d")
                    pool.indirect_dma_start(dst, bass.IndirectOffsetOnAxis(ap=token_i[:, r:r + 1], axis=0), f_y[r], None,
                                            bounds_check=NB * S - 1, oob_is_err=False).then_inc(y_scattered[r], 16)

                for i in range(4):
                    rstd_tile(i)
                loop(pool, SLOT_TILES, scatter_tile, unroll=RING)


        @block.scalar
        def _(act):

            for L in (0, 1):
                U = ATT[L]["units"]
                act.wait_ge(const_loaded, consts_there[L])
                if L == 1:
                    act.activation(bq[:], bq[:], ACT.Copy, scale=(D // ATT[1]["H"]) ** -0.5).then_inc(bq_done, 1)
                    act.wait_ge(bq_done, 1)

                def xT_evac(b):
                    act.wait_ge(A["xT_ps", L], b + 1)
                    wait(act, A["q_ps", L], b)
                    wait(act, R["lg_ps", L], b - 2 if L == 0 else b - 3)
                    act.activation(xT.rearrange("p a b -> p (a b)"), ps[:, 7, :], ACT.Copy).then_inc(A["xT_sb", L], 1)

                def cT_evac(b):
                    act.wait_ge(A["cT_ps", L], b + 1)
                    wait(act, A["kv_ps", L], b)
                    act.activation(cT.rearrange("p a b -> p (a b)"), ps[:, 7, 0:NC * Z], ACT.Copy).then_inc(A["cT_sb", L], 1)

                def q_evac(b):
                    act.wait_ge(A["q_ps", L], b + 1)
                    wait(act, A["s_ps", L], U * b)
                    for f in range(NC):
                        ins = act.activation(qT[:, f, :], ps[:, 7, f * S:(f + 1) * S], ACT.Identity, bias=bq[:, f:f + 1],
                                             scale=1.0 if L == 0 else (D // ATT[1]["H"]) ** -0.5)
                    ins.then_inc(A["q_sb", L], 1)

                def exp_unit(b, u):
                    n = U * b + u
                    act.wait_ge(A["sub_done", L], n + 1)
                    act.activation(p_sb[u % 2], p_sb[u % 2], ACT.Exp).then_inc(A["exp_done", L], 1)

                def pt_evac(b, u):
                    n = U * b + u
                    for g in range(2):
                        act.wait_ge(A["pt_ps", L], 2 * n + g + 1)
                        if g == 0:
                            wait(act, A["av_ps", L], n)
                        act.activation(pt_sb[g].rearrange("p a b -> p (a b)"), ps[0:Z, 4 + g, :], ACT.Copy
                                       ).then_inc(A["pt_sb", L], 1)

                def exp_gap(k):
                    act.wait_ge(R["gap_done", 0], k + 1)
                    act.activation(gate_new[:], gate_new[:], ACT.Exp).then_inc(R["gate_exp", 0], 1)

                def attnT_evac(b, j):
                    act.wait_ge(A["at_ps", L], TPB * b + j + 1)
                    wait(act, A["wo_ps", L], TPB * b + j)
                    act.activation(attnT.rearrange("p a b -> p (a b)"), ps[:, 7, 0:D], ACT.Copy).then_inc(A["at_sb", L], 1)

                def rT_evac(k):
                    act.wait_ge(R["xT_ps", L], k + 1)
                    wait(act, A["q_ps", L], upto(k + (3 if L == 0 else 4), NB))
                    wait(act, R["lg_ps", L], k)
                    act.activation(xT.rearrange("p a b -> p (a b)"), ps[:, 7, :], ACT.Copy).then_inc(R["xT_sb", L], 1)

                cT_evac(0)
                xT_evac(0)
                q_evac(0)
                if L == 0:
                    act.wait_ge(late_loaded, late_there[0])
                    act.activation(tg[:], tg[:], ACT.Tanh).then_inc(tanh_done, 1)
                    act.wait_ge(zeros_made, 1)
                    act.dma_start(slots_dram[E * REGION:NROWS, :].rearrange("(n p) d -> p n d", p=P),
                                  pad_rows[:].unsqueeze(1).broadcast_to([P, SLOT_TILES - MIN_TILES, ROW])).then_inc(zero_stored, 16)
                exp_unit(0, 0)
                if L == 1:
                    exp_unit(0, 1)
                    xT_evac(1)
                    cT_evac(1)
                    q_evac(1)

                def batch0(b, _r, _m):
                    nxt = before(b, NB - 1)
                    if since(b, 2):
                        rT_evac(b - 2)
                    pt_evac(b, 0)
                    if not isinstance(b, int) or b > 0:
                        attnT_evac(b - 1, 1)
                    exp_unit(b, 1)
                    exp_unit(b, 2)
                    pt_evac(b, 1)
                    if nxt:
                        xT_evac(b + 1)
                        cT_evac(b + 1)
                    exp_unit(b, 3)
                    if nxt:
                        q_evac(b + 1)
                    pt_evac(b, 2)
                    if since(b, 2):
                        exp_gap(b - 2)
                    attnT_evac(b, 0)
                    pt_evac(b, 3)
                    if nxt:
                        exp_unit(b + 1, 0)

                def batch1(b, _r, _m):
                    pt_evac(b, 0)
                    if since(b, 2):
                        rT_evac(b - 2)
                    if before(b, NB - 2):
                        xT_evac(b + 2)
                    if before(b, NB - 1):
                        exp_unit(b + 1, 0)
                    if before(b, NB - 2):
                        cT_evac(b + 2)
                    pt_evac(b, 1)
                    if before(b, NB - 2):
                        q_evac(b + 2)
                    if before(b, NB - 1):
                        exp_unit(b + 1, 1)

                if L == 0:
                    loop(act, NB, batch0, head=3)
                    rT_evac(NB - 2)
                    attnT_evac(NB - 1, 1)
                    rT_evac(NB - 1)
                    exp_gap(NB - 2)
                    exp_gap(NB - 1)
                else:
                    loop(act, NB, batch1, head=3, tail=2)
                    rT_evac(NB - 2)
                    rT_evac(NB - 1)

                act.wait_ge(R["pads_known", L], 1)
                act.wait_ge(zeros_made, 1)
                store_pads(act, L, range(1, E, 2))

                half = HIDDEN[L] // P // 2

                def expert_of(i):
                    return act.value_load(tile_expert[0:1, bass.ds(i, 1)], min_val=0, max_val=E - 1)

                def copy_w1(i, h, e):
                    wait(act, F["h_ps", L], 2 * (i - 1) + h + 1)
                    cols = slice(h * half * P, (h + 1) * half * P)
                    act.activation(w1_tile[:, :, cols], w1sb[:, bass.ds(e * NC, NC), cols], ACT.Copy
                                   ).then_inc(F["w1b_done" if h else "w1a_done", L], 1)

                def copies(i):
                    e = expert_of(i)
                    if L == 1:
                        copy_w1(i, 0, e)
                    copy_w1(i, 1, e)

                def xT_evac(i):
                    act.wait_ge(F["xT_ps", L], i + 1)
                    wait(act, F["h_ps", L], 2 * i)
                    act.activation(f_xT.rearrange("p a b -> p (a b)"), ps[:, 7, 0:D], ACT.Copy).then_inc(F["xT_sb", L], 1)

                def gelus(i, r):
                    e = expert_of(i)
                    wait(act, F["y_ps", L], i)
                    for h in range(2):
                        act.wait_ge(F["h_ps", L], 2 * i + h + 1)
                        for n in range(h * half, (h + 1) * half):
                            ins = act.activation(f_hT[:, n, :], ps[:, 2 * r + n // 4, (n % 4) * P:(n % 4 + 1) * P], ACT.Gelu,
                                                 bias=b1T[:, n, bass.ds(e, 1)])
                        ins.then_inc(F["hT_sb", L], 1)

                act.wait_ge(R["routed", L], 1)
                act.wait_ge(weights_loaded[L], 16 * 2 * NB)
                copies(0)
                xT_evac(0)
                copies(1)

                def tile(i, r, _m):
                    if before(i, SLOT_TILES - 1):
                        xT_evac(i + 1)
                    gelus(i, r)
                    if before(i, SLOT_TILES - 2):
                        copies(i + 2)

                loop(act, SLOT_TILES, tile, unroll=H_RING)

        @block.tensor
        def _(pe):
            pe.wait_ge(const_made, 2)
            for L in (0, 1):
                U, H, hpc = (ATT[L][k] for k in ("units", "H", "hpc"))
                d = D // H

                def turn_x(b):
                    pe.wait_ge(A["xhat_done", L], b + 1)
                    wait(pe, A["v_evac", L], 1 if isinstance(b, int) and b == 0 else b)
                    if L == 0:
                        wait(pe, A["res_done", 0], TPB * (b - 1))
                    else:
                        wait(pe, R["xT_sb", L], b - 3)
                    for c in range(NC):
                        for j in range(TPB):
                            ins = pe.transpose(ps[:, 7, c * S + j * P:c * S + (j + 1) * P], xhat[:, j, c * P:(c + 1) * P], ident[:])
                    ins.then_inc(A["xT_ps", L], 1)

                def turn_ctx(b):
                    pe.wait_ge(A["ctx_loaded", L], 16 * b + 16)
                    if since(b, 1):
                        pe.wait_ge(A["xT_sb", L], b + 1)
                    for c in range(NC):
                        ins = pe.transpose(ps[:, 7, c * Z:(c + 1) * Z], ctxs[:, c * P:(c + 1) * P], ident[0:Z, 0:Z])
                    ins.then_inc(A["cT_ps", L], 1)

                def project_q(b):
                    pe.wait_ge(A["cT_sb", L], b + 1)
                    pe.wait_ge(A["xT_sb", L], b + 1)
                    for f in range(NC):
                        for k in range(NC):
                            ins = pe.matmul(ps[:, 7, f * S:(f + 1) * S], wq[:, k, f * P:(f + 1) * P], xT[:, k, :],
                                            start=(k == 0), stop=(k == NC - 1))
                    ins.then_inc(A["q_ps", L], 1)

                def project_kv(b):
                    if since(b, 1):
                        pe.wait_ge(A["q_sb", L], b + 1)
                    else:
                        pe.wait_ge(A["cT_sb", L], 1)
                        pe.wait_ge(const_loaded, consts_there[L])
                    for f in range(NC):
                        for k in range(NC):
                            pe.matmul(ps[:, 7, f * Z:(f + 1) * Z], wk[:, k, f * P:(f + 1) * P], cT[:, k, :],
                                      start=(k == 0), stop=(k == NC - 1))
                    for k in range(NC):
                        ins = pe.matmul(ps[0:Z, 7, D:2 * D], cT[:, k, :], wv[:, k, :], start=(k == 0), stop=(k == NC - 1))
                    ins.then_inc(A["kv_ps", L], 1)

                def scores(b, u):
                    n, buf = U * b + u, u % 2
                    if u == 0:
                        pe.wait_ge(A["kbd_done", L], b + 1)
                        pe.wait_ge(A["q_sb", L], b + 1)
                    wait(pe, A["sub_done", L], n - 1)
                    if L == 0 and u == 1:
                        wait(pe, R["lg_done", L], b - 2)
                    for g in range(2):
                        if L == 0:
                            lhs, rhs = qT[:, u % 2, (u // 2) * P:(u // 2 + 1) * P], kbd[:, u % 2, g * GZ:(g + 1) * GZ]
                        else:
                            lhs, rhs = qT[:, g, u * P:(u + 1) * P], kbd[:, g, 0:GZ]
                        ins = pe.matmul(ps[:, 2 * buf + g, 0:GZ], lhs, rhs, start=True, stop=True)
                    ins.then_inc(A["s_ps", L], 1)

                def turn_p(b, u):
                    n = U * b + u
                    pe.wait_ge(A["exp_done", L], n + 1)
                    for g in range(2):
                        wait(pe, A["pt_sb", L], 2 * n + g - 1)
                        for k in range(HG):
                            ins = pe.transpose(ps[0:Z, 4 + g, k * P:(k + 1) * P], p_sb[u % 2][:, g, k * Z:(k + 1) * Z], ident[:])
                        ins.then_inc(A["pt_ps", L], 1)

                def weigh_v(b, u):
                    n = U * b + u
                    j, first = (u // 2, u % 2 == 0) if L == 0 else (u, True)
                    if u == 0:
                        pe.wait_ge(A["v_done", L], b + 1)
                    if first:
                        wait(pe, A["attn_done", L], TPB * b + j)
                    for g in range(2):
                        pe.wait_ge(A["pt_sb", L], 2 * n + g + 1)
                        for k in range(HG):
                            h = (u % 2) * 8 + g * HG + k if L == 0 else g * HG + k
                            ins = pe.matmul(ps[:, 6, h * (d + 1):(h + 1) * (d + 1)], pt_sb[g][:, k, :],
                                            vaug[:, h * (d + 1):(h + 1) * (d + 1)], start=True, stop=True)
                    ins.then_inc(A["av_ps", L], 1)

                def turn_attn(b, j):
                    if j == 0 and before(b, NB - 1):
                        pe.wait_ge(A["v_evac", L], b + 2)
                    else:
                        wait(pe, A["res_done", L], TPB * b + j)
                    if j == 1:
                        wait(pe, R["xT_sb", L], upto(b, NB - 1))
                    pe.wait_ge(A["attn_done", L], TPB * b + j + 1)
                    for c in range(NC):
                        ins = pe.transpose(ps[:, 7, c * P:(c + 1) * P], attn[:, c * P:(c + 1) * P], ident[:])
                    ins.then_inc(A["at_ps", L], 1)

                def project_out(b, j):
                    pe.wait_ge(A["at_sb", L], TPB * b + j + 1)
                    for k in range(NC):
                        ins = pe.matmul(ps[:, 7, 0:D], attnT[:, k, :], wo[:, k, :], start=(k == 0), stop=(k == NC - 1))
                    ins.then_inc(A["wo_ps", L], 1)

                def turn_rows(k):
                    pe.wait_ge(R["x_done", L], k + 1)
                    if L == 0:
                        wait(pe, A["res_done", L], upto(TPB * (k + 1) + 1, NT))
                    else:
                        wait(pe, A["v_evac", L], upto(k + 4, NB))
                    wait(pe, R["xT_sb", L], k)
                    for c in range(NC):
                        for j in range(TPB):
                            ins = pe.transpose(ps[:, 7, c * S + j * P:c * S + (j + 1) * P], r_x[:, j, c * P:(c + 1) * P], ident[:])
                    ins.then_inc(R["xT_ps", L], 1)

                def route(k):
                    wait(pe, A["sub_done", L], upto(U * (k + 2) + 2, U * NB))
                    wait(pe, R["lg_done", L], k)
                    if before(k, NB):
                        pe.wait_ge(R["xT_sb", L], k + 1)
                        for j in range(TPB):
                            for c in range(NC):
                                ins = pe.matmul(ps[:, 2, LG0 + j * E:LG0 + (j + 1) * E], xT[:, c, j * P:(j + 1) * P], wr[:, c, :],
                                                start=(c == 0), stop=(c == NC - 1))
                    if since(k, 1):
                        pe.wait_ge(R["onehot_done", L], k)
                        flat = one_hot[:].rearrange("p a b -> p (a b)")
                        for j in range(TPB):
                            for q in range(j + 1):
                                pe.matmul(ps[:, 2, RK0 + j * E:RK0 + (j + 1) * E], (upper if q == j else ones_b)[:],
                                          flat[:, q * E:(q + 1) * E], start=(q == 0), stop=(q == j))
                        for q in range(TPB):
                            ins = pe.matmul(ps[:, 2, CT0:CT0 + E], ones_b[:], flat[:, q * E:(q + 1) * E],
                                            start=(q == 0), stop=(q == TPB - 1))
                    ins.then_inc(R["lg_ps", L], 1)

                turn_ctx(0)
                project_kv(0)
                turn_x(0)
                project_q(0)
                scores(0, 0)
                scores(0, 1)
                pe.wait_ge(bias_loaded, 16 * 4 * (L + 1))
                for n in range(HIDDEN[L] // P):
                    ins = pe.transpose(ps[:, 6, n * E:(n + 1) * E], b1_rows[L][:, n * P:(n + 1) * P], ident[0:E, 0:E])
                ins.then_inc(b1_turned, 1)
                pe.wait_ge(late_loaded, late_there[L])
                if L == 1:
                    turn_x(1)
                    turn_ctx(1)
                    project_q(1)
                    project_kv(1)
                pe.wait_ge(bias_split, L + 1)

                def batch0(b, _r, _m):
                    nxt, past = before(b, NB - 1), not isinstance(b, int) or b > 0
                    turn_p(b, 0)
                    scores(b, 2)
                    if past:
                        turn_attn(b - 1, 1)
                    weigh_v(b, 0)
                    if past:
                        project_out(b - 1, 1)
                    turn_p(b, 1)
                    if since(b, 2):
                        route(b - 2)
                    if nxt:
                        turn_x(b + 1)
                    scores(b, 3)
                    if nxt:
                        turn_ctx(b + 1)
                    weigh_v(b, 1)
                    if nxt:
                        project_q(b + 1)
                    turn_p(b, 2)
                    if nxt:
                        project_kv(b + 1)
                    weigh_v(b, 2)
                    if nxt:
                        scores(b + 1, 0)
                    turn_attn(b, 0)
                    turn_p(b, 3)
                    if nxt:
                        scores(b + 1, 1)
                    project_out(b, 0)
                    weigh_v(b, 3)
                    if past:
                        turn_rows(b - 1)

                def batch1(b, _r, _m):
                    turn_p(b, 0)
                    if before(b, NB - 1):
                        scores(b + 1, 0)
                    if since(b, 2):
                        turn_rows(b - 2)
                    weigh_v(b, 0)
                    if since(b, 2):
                        route(b - 2)
                    if before(b, NB - 2):
                        turn_x(b + 2)
                    turn_p(b, 1)
                    if before(b, NB - 2):
                        turn_ctx(b + 2)
                    if before(b, NB - 1):
                        scores(b + 1, 1)
                    if before(b, NB - 2):
                        project_q(b + 2)
                    weigh_v(b, 1)
                    if before(b, NB - 2):
                        project_kv(b + 2)

                if L == 0:
                    loop(pe, NB, batch0, head=3)
                    turn_attn(NB - 1, 1)
                    project_out(NB - 1, 1)
                    route(NB - 2)
                else:
                    loop(pe, NB, batch1, head=3, tail=2)
                    turn_rows(NB - 2)
                    route(NB - 2)
                turn_rows(NB - 1)
                route(NB - 1)
                route(NB)

                KC = HIDDEN[L] // P
                half = KC // 2
                pe.wait_ge(weights_loaded[L], 16 * 2 * NB)
                pe.wait_ge(R["routed", L], 1)

                def f_turn(i):
                    pe.wait_ge(F["x_done", L], i + 1)
                    wait(pe, F["xT_sb", L], i)
                    for c in range(NC):
                        ins = pe.transpose(ps[:, 7, c * P:(c + 1) * P], f_xn[:, c * P:(c + 1) * P], ident[:])
                    ins.then_inc(F["xT_ps", L], 1)

                def flat(ap):
                    return ap.rearrange("p a b -> p (a b)")

                def hidden(i, r):
                    pe.wait_ge(F["xT_sb", L], i + 1)
                    wait(pe, F["hT_sb", L], 2 * (i - H_RING) + 2)
                    for h in range(2):
                        pe.wait_ge(F["w1b_done" if h else "w1a_done", L], i + 1)
                        for n in range(h * half, (h + 1) * half):
                            for k in range(NC):
                                ins = pe.matmul(ps[:, 2 * r + n // 4, (n % 4) * P:(n % 4 + 1) * P], w1_tile[:, k, n * P:(n + 1) * P],
                                                f_xT[:, k, :], start=(k == 0), stop=(k == NC - 1))
                        ins.then_inc(F["h_ps", L], 1)

                def down(i):
                    e = pe.value_load(tile_expert[0:1, bass.ds(i, 1)], min_val=0, max_val=E - 1)
                    wait(pe, F["y_sb", L], i)
                    pe.matmul(ps[:, 6, 0:D], flat(expert_rows[:, bass.ds(e, 1), :]), b2w[:], start=True, stop=False)
                    for k in range(KC):
                        if k % half == 0:
                            pe.wait_ge(F["hT_sb", L], 2 * i + k // half + 1)
                        ins = pe.matmul(ps[:, 6, 0:D], f_hT[:, k, :], flat(w2sb[:, bass.ds(e * KC + k, 1), :]),
                                        start=False, stop=(k == KC - 1))
                    ins.then_inc(F["y_ps", L], 1)

                f_turn(0)
                hidden(0, 0)
                f_turn(1)

                def tile(i, r, _m):
                    if before(i, SLOT_TILES - 1):
                        hidden(i + 1, (r + 1) % H_RING)
                    if before(i, SLOT_TILES - 2):
                        f_turn(i + 2)
                    down(i)

                loop(pe, SLOT_TILES, tile, unroll=H_RING)

        @block.vector
        def _(dve):
            def split_bias(L):
                f, w, n = b2_rows[L], b2w[:], HIDDEN[L] // P
                dve.wait_ge(b1_turned, L + 1)
                dve.tensor_copy(b1T[:, 0:n, :].rearrange("p a b -> p (a b)"), ps[:, 6, 0:n * E])
                ch = Chain(dve, bias_link)
                ch.begin(4 * L)
                link = ch.link
                link(dve.tensor_copy(w, f))
                link(dve.tensor_tensor(f, f, w, ALU.subtract))
                dve.tensor_copy(w[32:64], f[32:64])
                link(dve.tensor_copy(w[64:96], f[64:96]))
                link(dve.tensor_tensor(f[64:96], f[64:96], w[64:96], ALU.subtract))
                dve.tensor_copy(w[64:96], f[64:96]).then_inc(bias_split, L + 1)

            dve.memset(b2_rows[0], 0.0).then_inc(bias_zeroed, 1)
            for L in (0, 1):
                U, H, hpc = (ATT[L][k] for k in ("units", "H", "hpc"))
                d = D // H
                prep = Chain(dve, A["prep_chain", L], wait_carried)
                sm_chain, norm_chain = Chain(dve, A["sm_chain", L]), Chain(dve, norm_link)
                sm_links = (2, 2, 1, 1) if L == 0 else (2, 2)
                hm = headmask[L]

                def row(t):
                    return xres[:, bass.ds(t, 1), 0:D].rearrange("p a d -> p (a d)")

                def prep_stats(b):
                    prep.begin(b)
                    dve.wait_ge(A["x_loaded", L], 16 * b + 16)
                    wait(dve, A["xhat_done", L], b)
                    dve.sem_inc(wait_carried, 1)
                    for j in range(TPB):
                        ins = dve.bn_stats(xst[:, j, :], row(TPB * b + j))
                    prep.link(ins)
                    for j in range(TPB):
                        ins = dve.bn_aggr(mv[:, j, :], xst[:, j, :])
                    ins.then_inc(A["stats_done", L], 1)

                def prep_apply(b):
                    dve.wait_ge(A["rstd_done", L], b + 1)
                    wait(dve, A["xT_ps", L], b)
                    for j in range(TPB):
                        ins = dve.tensor_scalar(xhat[:, j, :], row(TPB * b + j), mv[:, j, 0:1], rstd[:, j:j + 1],
                                                ALU.subtract, ALU.mult)
                    ins.then_inc(A["xhat_done", L], 1)

                def scale_mask(b):
                    dve.wait_ge(A["mask_loaded", 1], 16 * b + 16)
                    dve.tensor_scalar(maskneg[:], rawmask, -ATT[1]["mask_val"], None, ALU.mult).then_inc(A["mask_done", 1], 1)

                def make_kbd(b):
                    dve.wait_ge(A["kv_ps", L], b + 1)
                    wait(dve, A["s_ps", L], U * b)
                    for c in range(NC):
                        ins = dve.scalar_tensor_tensor(
                            out=kbd[:, c, 0:hpc * Z].rearrange("p (h z) -> p h z", h=hpc),
                            in0=ps[:, 7, c * Z:(c + 1) * Z].unsqueeze(1).broadcast_to([P, hpc, Z]), scalar=bk[:, c:c + 1],
                            in1=hm[:].unsqueeze(2).broadcast_to([P, hpc, Z]), op0=ALU.add, op1=ALU.mult)
                    ins.then_inc(A["kbd_done", L], 1)

                def make_v(b):
                    wait(dve, A["v_done", L], b)
                    dve.tensor_tensor(vnext[:, 0:H * (d + 1)].rearrange("p (h e) -> p h e", h=H)[:, :, 0:d],
                                      ps[0:Z, 7, D:2 * D].rearrange("p (h e) -> p h e", h=H),
                                      bv[:].rearrange("p (h e) -> p h e", h=H), ALU.add).then_inc(A["v_evac", L], 1)

                def softmax_unit(b, u):
                    n, buf = U * b + u, u % 2
                    sm_chain.begin(sum(sm_links) * b + sum(sm_links[:u]))
                    dve.wait_ge(A["s_ps", L], n + 1)
                    wait(dve, A["pt_ps", L], 2 * (n - 1))
                    src = ps[:, 2 * buf:2 * buf + 2, 0:GZ].rearrange("p g (k z) -> p g k z", k=HG)
                    dst = p_sb[buf].rearrange("p g (k z) -> p g k z", k=HG)
                    j = u // 2 if L == 0 else u
                    if sm_links[u] == 2:
                        if L == 1 and u == 0:
                            dve.wait_ge(A["mask_done", 1], b + 1)
                        m = maskneg[:, j, :].unsqueeze(1).unsqueeze(1).broadcast_to([P, 2, HG, Z])
                        sm_chain.link(dve.tensor_tensor(dst, src, m, ALU.add))
                        src = dst
                    m8 = mx.rearrange("p (g k) -> p g k", g=2)
                    wait(dve, A["sub_done", L], n)
                    sm_chain.link(dve.tensor_reduce(m8, src, AX, ALU.max))
                    dve.tensor_tensor(dst, src, m8.unsqueeze(3).broadcast_to([P, 2, HG, Z]), ALU.subtract
                                      ).then_inc(A["sub_done", L], 1)

                def normalise(b, j):
                    norm_chain.begin(TPB * (b + NB * L) + j)
                    dve.wait_ge(A["av_ps", L], U * b + (2 * j + 2 if L == 0 else j + 1))
                    av = ps[:, 6, 0:H * (d + 1)].rearrange("p (h e) -> p h e", h=H)
                    wait(dve, A["attn_done", L], TPB * b + j)
                    norm_chain.link(dve.reciprocal(rinv[:, 0:H].unsqueeze(2), av[:, :, d:d + 1]))
                    if L == 0:
                        wait(dve, A["at_ps", 0], TPB * b + j)
                    else:
                        wait(dve, A["res_done", 1], TPB * b + j)
                    ins = dve.tensor_tensor(attn.rearrange("p (h e) -> p h e", h=H), av[:, :, 0:d],
                                            rinv[:, 0:H].unsqueeze(2).broadcast_to([P, H, d]), ALU.mult)
                    ins.then_inc(A["attn_done", L], 1)
                    if L == 1:
                        dve.wait_ge(A["attn_done", 1], TPB * b + j + 1)
                        t = row(TPB * b + j)
                        dve.scalar_tensor_tensor(out=t, in0=attn, scalar=tg[:, 1:2], in1=t, op0=ALU.mult, op1=ALU.add
                                                 ).then_inc(A["res_done", 1], 1)

                def residual(b, j):
                    dve.wait_ge(A["wo_ps", L], TPB * b + j + 1)
                    t = row(TPB * b + j)
                    dve.scalar_tensor_tensor(out=t, in0=ps[:, 7, 0:D], scalar=tg[:, 0:1], in1=t, op0=ALU.mult, op1=ALU.add
                                             ).then_inc(A["res_done", L], 1)

                rch = Chain(dve, rows_link, wait_carried)
                ch = Chain(dve, R["route_chain", L])
                route_links = 7 if L == 0 else 5

                def row_stats(k):
                    rch.begin(k + NB * L)
                    wait(dve, R["x_done", L], k)
                    if L == 0:
                        dve.wait_ge(A["bo_done", 0], TPB * k + TPB)
                    else:
                        dve.wait_ge(A["res_done", 1], TPB * k + TPB)
                    dve.sem_inc(wait_carried, 1)
                    for j in range(TPB):
                        ins = dve.bn_stats(r_st[:, j, :], row(TPB * k + j))
                    rch.link(ins)
                    for j in range(TPB):
                        ins = dve.bn_aggr(r_mv[:, j, :], r_st[:, j, :])
                    ins.then_inc(R["stats_done", L], 1)

                def row_apply(k):
                    dve.wait_ge(R["rstd_done", L], k + 1)
                    wait(dve, R["xT_ps", L], k)
                    for j in range(TPB):
                        ins = dve.tensor_scalar(r_x[:, j, :], row(TPB * k + j), r_mv[:, j, 0:1], r_rstd[:, j:j + 1],
                                                ALU.subtract, ALU.mult)
                    ins.then_inc(R["x_done", L], 1)

                def over_e(ap):
                    return ap.unsqueeze(2).broadcast_to([P, TPB, E])

                def over_t(ap):
                    return ap.unsqueeze(1).broadcast_to([P, TPB, E])

                def bank2(at, n):
                    return ps[:, 2, at:at + n]

                def choose(k):
                    new, old = before(k, NB), since(k, 1)
                    ch.begin(route_links * k)
                    dve.wait_ge(R["lg_ps", L], k + 1)
                    if new:
                        ins = dve.tensor_tensor(lg, bank2(LG0, TPB * E).rearrange("p (t e) -> p t e", e=E), over_t(brb[:]), ALU.add)
                    if old:
                        ins = dve.tensor_tensor(slot_of, bank2(RK0, TPB * E).rearrange("p (t e) -> p t e", e=E), over_t(row_base[:]), ALU.add)
                        ch.link(ins)
                        dve.tensor_tensor(row_base[:], row_base[:], bank2(CT0, E), ALU.add).then_inc(R["lg_done", L], 1)
                        if L == 0:
                            dve.wait_ge(R["gate_exp", 0], k)
                            dve.tensor_scalar(gate_new[:], gate_new[:], 1.0, None, ALU.add)
                        ins = dve.tensor_tensor(slot_of, slot_of, one_hot[:], ALU.mult)
                    else:
                        ins.then_inc(R["lg_done", L], 1)
                        dve.wait_ge(R["lg_done", L], 1)
                        ch.link(dve.memset(slot_of, 0.0))
                    if new:
                        ins = dve.tensor_reduce(tmax, lg, AX, ALU.max)
                    ch.link(ins)
                    if old:
                        if L == 0:
                            dve.reciprocal(gate_new[:], gate_new[:])
                        ins = dve.tensor_reduce(slot_f, slot_of, AX, ALU.add)
                    if new:
                        ins = dve.tensor_tensor(is_top, lg, over_e(tmax), ALU.is_equal)
                    ch.link(ins)
                    if L == 0 and old:
                        dve.tensor_scalar(xres[:, bass.ds(TPB * (k - 1), TPB), D], gate_new[:], tg[:, 2:3], None, ALU.mult)
                    if old:
                        dve.tensor_copy(slot_i[:, bass.ds(TPB * (k - 1), TPB)], slot_f).then_inc(R["slot_done", L], 1)
                    if not new:
                        return
                    ch.link(dve.tensor_tensor(is_top, is_top, over_t(exp_rev[:]), ALU.mult))
                    ch.link(dve.tensor_reduce(tmax2, is_top, AX, ALU.max))
                    dve.tensor_tensor(one_hot[:], is_top, over_e(tmax2), ALU.is_equal).then_inc(R["onehot_done", L], 1)
                    if L == 0:
                        dve.wait_ge(R["onehot_done", L], k + 1)
                        ch.link(dve.scalar_tensor_tensor(out=is_top, in0=one_hot[:], scalar=-3.0e38, in1=lg, op0=ALU.mult, op1=ALU.add))
                        ch.link(dve.tensor_reduce(tmax2, is_top, AX, ALU.max))
                        dve.tensor_tensor(gate_new[:], tmax2, tmax, ALU.subtract).then_inc(R["gap_done", 0], 1)

                if L == 0:
                    dve.wait_ge(const_made, 2)
                else:
                    dve.wait_ge(F["y_sb", 0], SLOT_TILES)
                    dve.memset(b2_rows[1], 0.0).then_inc(bias_zeroed, 1)
                dve.memset(vnext, 1.0).then_inc(vaug_ones, 1)
                dve.wait_ge(vaug_ones, L + 1)
                if L == 0:
                    prep_stats(0)
                    prep_apply(0)
                dve.wait_ge(const_loaded, consts_there[L])
                make_kbd(0)
                make_v(0)
                if L == 1:
                    rows_back(dve, 0)
                    prep_stats(0)
                    prep_apply(0)
                    scale_mask(0)
                    prep_stats(1)
                    prep_apply(1)
                softmax_unit(0, 0)
                if L == 1:
                    softmax_unit(0, 1)
                    scale_mask(1)
                    prep_stats(2)
                    make_kbd(1)
                    make_v(1)
                split_bias(L)

                def batch0(b, _r, _m):
                    nxt, past = before(b, NB - 1), not isinstance(b, int) or b > 0
                    softmax_unit(b, 1)
                    softmax_unit(b, 2)
                    if nxt:
                        prep_apply(b + 1)
                    if past:
                        residual(b - 1, 1)
                    softmax_unit(b, 3)
                    normalise(b, 0)
                    if past:
                        row_stats(b - 1)
                    if since(b, 2):
                        choose(b - 2)
                    if nxt:
                        make_kbd(b + 1)
                        make_v(b + 1)
                        softmax_unit(b + 1, 0)
                    if before(b, NB - 2):
                        prep_stats(b + 2)
                    residual(b, 0)
                    if past:
                        row_apply(b - 1)
                    normalise(b, 1)

                def batch1(b, _r, _m):
                    if before(b, NB - 2):
                        prep_apply(b + 2)
                    if before(b, NB - 1):
                        softmax_unit(b + 1, 0)
                    if since(b, 1):
                        row_stats(b - 1)
                    normalise(b, 0)
                    if before(b, NB - 1):
                        softmax_unit(b + 1, 1)
                    if since(b, 1):
                        row_apply(b - 1)
                    if before(b, NB - 2):
                        scale_mask(b + 2)
                    if before(b, NB - 3):
                        prep_stats(b + 3)
                    if before(b, NB - 2):
                        make_kbd(b + 2)
                        make_v(b + 2)
                    normalise(b, 1)
                    if since(b, 2):
                        choose(b - 2)

                if L == 0:
                    dve.wait_ge(tanh_done, 1)
                    prep_stats(1)
                    loop(dve, NB, batch0, unroll=2, head=2)
                    residual(NB - 1, 1)
                else:
                    loop(dve, NB, batch1, unroll=2, head=2, tail=2)

                row_stats(NB - 1)
                row_apply(NB - 1)
                choose(NB - 2)
                choose(NB - 1)
                choose(NB)
                dve.wait_ge(R["lg_done", L], NB + 1)
                dve.wait_ge(R["slot_done", L], NB)
                link = ch.link
                dve.tensor_copy(pad_row[:], row_base[0:1]).then_inc(R["pads_known", L], 1)
                dve.memset(ones8, 1.0)
                link(dve.tensor_tensor(total, row_base[:], region0[:], ALU.subtract))
                link(dve.tensor_tensor(steps_below, total.unsqueeze(2).broadcast_to([P, E, NT]),
                                       steps128[:].unsqueeze(1).broadcast_to([P, E, NT]), ALU.is_gt))
                link(dve.tensor_reduce(tiles, steps_below, AX, ALU.add))
                link(dve.tensor_tensor_scan(tend, ones8, tiles, 0.0, ALU.mult, ALU.add))
                dve.tensor_scalar(delta, tiles, -float(P), float(REGION), ALU.mult, ALU.add)
                link(dve.tensor_tensor(te_cmp, tile_no[:].unsqueeze(2).broadcast_to([1, 40, E]),
                                       tend[0:1].unsqueeze(1).broadcast_to([1, 40, E]), ALU.is_ge))
                dve.tensor_reduce(te_sum, te_cmp, AX, ALU.add)
                link(dve.scalar_tensor_tensor(out=delta[:, E - 1:E], in0=tend[:, E - 1:E], scalar=float(P),
                                              in1=delta[:, E - 1:E], op0=ALU.mult, op1=ALU.add))
                dve.tensor_scalar(tile_expert[:], te_sum, float(E - 1), None, ALU.min)
                link(dve.tensor_scalar(delta[:, E - 1:E], delta[:, E - 1:E], -float(MIN_TILES * P), None, ALU.add))
                link(dve.tensor_tensor(te_cmp, te_cmp, delta[0:1].unsqueeze(1).broadcast_to([1, 40, E]), ALU.mult))
                link(dve.tensor_reduce(te_sum, te_cmp, AX, ALU.add))
                link(dve.scalar_tensor_tensor(out=tile_row[:], in0=tile_no[:], scalar=float(P), in1=te_sum, op0=ALU.mult,
                                              op1=ALU.add))
                dve.tensor_copy(row_base[:], region0[:]).then_inc(R["routed", L], 1)

                half = HIDDEN[L] // P // 2
                fch = Chain(dve, experts_link, wait_carried)

                def copy_w1(i):
                    if L == 0:
                        e = dve.value_load(tile_expert[0:1, bass.ds(i, 1)], min_val=0, max_val=E - 1)
                        wait(dve, F["h_ps", L], 2 * (i - 1) + 1)
                        dve.tensor_copy(w1_tile[:, :, 0:half * P], w1sb[:, bass.ds(e * NC, NC), 0:half * P]
                                        ).then_inc(F["w1a_done", L], 1)

                def f_stats(i, r, m):
                    fch.begin(i + SLOT_TILES * L)
                    wait(dve, F["x_done", L], i)
                    dve.wait_ge(xs_loaded[r], 16 * (m + 1 + uses(r) * L))
                    dve.sem_inc(wait_carried, 1)
                    fch.link(dve.bn_stats(f_st, xs[r][:, 0:D]))
                    dve.bn_aggr(f_mv, f_st).then_inc(F["stats_done", L], 1)

                def f_apply(i, r):
                    dve.wait_ge(F["rstd_done", L], i + 1)
                    wait(dve, F["xT_ps", L], i)
                    dve.tensor_scalar(f_xn, xs[r][:, 0:D], f_mv[:, 0:1], f_rstd, ALU.subtract, ALU.mult).then_inc(F["x_done", L], 1)

                def finish(i, r, m):
                    wait(dve, y_scattered[r], 16 * (m + uses(r) * L))
                    dve.tensor_copy(token_i[:, r:r + 1], xs[r][:, D + 1:ROW])
                    dve.wait_ge(F["y_ps", L], i + 1)
                    dve.scalar_tensor_tensor(out=f_y[r], in0=ps[:, 6, 0:D], scalar=xs[r][:, D:D + 1] if L == 0 else tg[:, 3:4],
                                             in1=xs[r][:, 0:D], op0=ALU.mult, op1=ALU.add).then_inc(F["y_sb", L], 1)

                dve.wait_ge(R["routed", L], 1)
                dve.wait_ge(weights_loaded[L], 16 * 2 * NB)
                copy_w1(0)
                for i in range(3):
                    f_stats(i, i, 0)
                    if i == 2:
                        copy_w1(1)
                    f_apply(i, i)
                f_stats(3, 3, 0)

                def tile(i, r, m):
                    if before(i, SLOT_TILES - 3):
                        f_apply(i + 3, (r + 3) % RING)
                    if before(i, SLOT_TILES - 4):
                        f_stats(i + 4, (r + 4) % RING, m + (r + 4) // RING)
                    if before(i, SLOT_TILES - 2):
                        copy_w1(i + 2)
                    finish(i, r, m)

                loop(dve, SLOT_TILES, tile, unroll=RING)


_INS = ['x', 'ctx_1024', 'mask_BxSxS2_ff0', 'g_xattn', 'g_ffn', 'L0_xattn_w_q', 'L0_xattn_b_q', 'L0_xattn_w_kv',
        'L0_xattn_b_kv', 'L0_xattn_w_out', 'L0_xattn_b_out', 'L0_ffn_w1', 'L0_ffn_b1', 'L0_ffn_w2', 'L0_ffn_b2',
        'L0_ffn_wr', 'L0_ffn_br', 'L1_xattn_wq_kernel', 'L1_xattn_wq_bias', 'L1_xattn_wk_kernel', 'L1_xattn_wk_bias',
        'L1_xattn_wv_kernel', 'L1_xattn_wv_bias', 'L1_ffn_Wg', 'L1_ffn_bg', 'L1_ffn_W1', 'L1_ffn_b1', 'L1_ffn_W2',
        'L1_ffn_b2']


def kernel(**inputs):
    import numpy as _np
    import concourse.bacc as _bacc
    from concourse import mybir as _mybir
    from concourse.bass_utils import run_bass_kernel_spmd as _run

    nc = _bacc.Bacc("TRN2", target_bir_lowering=False, num_devices=1)
    arrays, args = {}, []
    for name in _INS:
        a = _np.ascontiguousarray(inputs[name])
        arrays[f"in_{name}_dram"] = a
        args.append(nc.dram_tensor(f"in_{name}_dram", a.shape, _mybir.dt.from_np(a.dtype), kind="ExternalInput").ap())
    args.append(nc.dram_tensor("out_0_dram", (NB, S, D), _mybir.dt.float32, kind="ExternalOutput").ap())
    flamingo_kernel(nc, *args)
    r = _run(nc, [arrays], core_ids=[0])
    return r.results[0]["out_0_dram"]
```
